# Optimizing a Trainium2 kernel written in Bass

```python
import numpy as np
import jax
import jax.numpy as jnp

def _softmax(x, axis=-1):
    return jax.nn.softmax(x, axis=axis)

def _gelu(x):
    return jax.nn.gelu(x, approximate=True)

def _silu(x):
    return jax.nn.silu(x)

def _sigmoid(x):
    return jax.nn.sigmoid(x)

def _layernorm(x, axis=-1, eps=1e-05):
    m = jnp.mean(x, axis=axis, keepdims=True)
    v = jnp.var(x, axis=axis, keepdims=True)
    return (x - m) / jnp.sqrt(v + eps)

def _scatter_add(tgt, idx, src, axis=0):
    return tgt.at[idx].add(src)

def _segment_sum(src, seg, n):
    return jax.ops.segment_sum(src, seg, n)
kernel_name = 'mk_adaln_d1_jaxref_r8_4c51af'

def setup_inputs(seed: int=0):
    np.random.seed(seed)
    _w = jnp.asarray

    def _L0_attn_setup():
        import jax, jax.numpy as jnp
        import numpy as np
        B_, S, H = (2, 256, 256)
        E = 2 * H
        P = 64
        NH = E // P
        N = 64
        G = 1
        K = 4
        CS = 32
        CONV_DIM = E + 2 * G * N
        PROJ = E + CONV_DIM + NH
        EPS = 1e-06

        def segment_sum(a):
            l = a.shape[-1]
            a_exp = jnp.broadcast_to(a[..., None], (*a.shape, l))
            a_exp = jnp.where(jnp.tril(jnp.ones((l, l), bool), -1), a_exp, 0.0)
            s = jnp.cumsum(a_exp, axis=-2)
            return jnp.where(jnp.tril(jnp.ones((l, l), bool), 0), s, -jnp.inf)
        key = jax.random.key(seed)
        ks = jax.random.split(key, 8)
        s = 0.02
        return {'x': jax.random.normal(ks[0], (B_, S, H), jnp.float32), 'in_proj_w': jax.random.normal(ks[1], (PROJ, H), jnp.float32) * s, 'conv_w': jax.random.normal(ks[2], (CONV_DIM, K), jnp.float32) * s, 'conv_b': jnp.zeros((CONV_DIM,), jnp.float32), 'dt_bias': jax.random.uniform(ks[3], (NH,), jnp.float32, 0.0, 1.0), 'A_log': jnp.log(jax.random.uniform(ks[4], (NH,), jnp.float32, 1.0, 16.0)), 'D': jnp.ones((NH,), jnp.float32), 'norm_w': jnp.ones((E,), jnp.float32), 'out_proj_w': jax.random.normal(ks[5], (H, E), jnp.float32) * s}
    _L0_attn_in = _L0_attn_setup()

    def _L0_ffn_setup():
        import jax, jax.numpy as jnp
        import numpy as np
        B, T, D = (2, 128, 256)
        E, F, K = (64, 64, 4)
        S, HS = (2, 64 * 4)
        key = jax.random.key(seed)
        ks = jax.random.split(key, 9)
        s = 0.02
        f32 = jnp.float32
        return {'x': jax.random.normal(ks[0], (B, T, D), f32), 'router_w': jax.random.normal(ks[1], (D, E), f32) * s, 'router_bias': jnp.zeros((E,), f32), 'wg': jax.random.normal(ks[2], (E, D, F), f32) * s, 'wu': jax.random.normal(ks[3], (E, D, F), f32) * s, 'wd': jax.random.normal(ks[4], (E, F, D), f32) * s, 'swg': jax.random.normal(ks[5], (S, D, HS), f32) * s, 'swu': jax.random.normal(ks[6], (S, D, HS), f32) * s, 'swd': jax.random.normal(ks[7], (S, HS, D), f32) * s}
    _L0_ffn_in = _L0_ffn_setup()
    _L0_c = _w((lambda *s: np.random.randn(*s).astype(np.float32) * 0.05)(1, 256))
    _L0_wmod = _w((lambda *s: np.random.randn(*s).astype(np.float32) * 0.05)(256, 6 * 256) * 256 ** (-0.5))
    _d = {'L0_attn_x': _L0_attn_in['x'], 'L0_attn_in_proj_w': _L0_attn_in['in_proj_w'], 'L0_attn_conv_w': _L0_attn_in['conv_w'], 'L0_attn_conv_b': _L0_attn_in['conv_b'], 'L0_attn_dt_bias': _L0_attn_in['dt_bias'], 'L0_attn_A_log': _L0_attn_in['A_log'], 'L0_attn_D': _L0_attn_in['D'], 'L0_attn_norm_w': _L0_attn_in['norm_w'], 'L0_attn_out_proj_w': _L0_attn_in['out_proj_w'], 'L0_ffn_router_w': _L0_ffn_in['router_w'], 'L0_ffn_router_bias': _L0_ffn_in['router_bias'], 'L0_ffn_wg': _L0_ffn_in['wg'], 'L0_ffn_wu': _L0_ffn_in['wu'], 'L0_ffn_wd': _L0_ffn_in['wd'], 'L0_ffn_swg': _L0_ffn_in['swg'], 'L0_ffn_swu': _L0_ffn_in['swu'], 'L0_ffn_swd': _L0_ffn_in['swd'], 'L0_c': _L0_c, 'L0_wmod': _L0_wmod}
    _x0 = _d['L0_attn_x']
    _d['L0_attn_x'] = jax.random.normal(jax.random.fold_in(jax.random.key(seed), 1), (1, 2048, 256), dtype=_x0.dtype)
    del _x0
    return _d

def reference(L0_attn_x, L0_attn_in_proj_w, L0_attn_conv_w, L0_attn_conv_b, L0_attn_dt_bias, L0_attn_A_log, L0_attn_D, L0_attn_norm_w, L0_attn_out_proj_w, L0_ffn_router_w, L0_ffn_router_bias, L0_ffn_wg, L0_ffn_wu, L0_ffn_wd, L0_ffn_swg, L0_ffn_swu, L0_ffn_swd, L0_c, L0_wmod):

    def _L0_attn_ref(x, in_proj_w, conv_w, conv_b, dt_bias, A_log, D, norm_w, out_proj_w):
        import jax, jax.numpy as jnp
        import numpy as np
        B_, S, H = (2, 256, 256)
        E = 2 * H
        P = 64
        NH = E // P
        N = 64
        G = 1
        K = 4
        CS = 32
        CONV_DIM = E + 2 * G * N
        PROJ = E + CONV_DIM + NH
        EPS = 1e-06

        def segment_sum(a):
            l = a.shape[-1]
            a_exp = jnp.broadcast_to(a[..., None], (*a.shape, l))
            a_exp = jnp.where(jnp.tril(jnp.ones((l, l), bool), -1), a_exp, 0.0)
            s = jnp.cumsum(a_exp, axis=-2)
            return jnp.where(jnp.tril(jnp.ones((l, l), bool), 0), s, -jnp.inf)
        b, s, _ = x.shape
        proj = x @ in_proj_w.T
        gate, hBC, dt = jnp.split(proj, [E, E + CONV_DIM], axis=-1)
        xp = jnp.pad(hBC, ((0, 0), (K - 1, 0), (0, 0)))
        conv = sum((xp[:, k:k + s, :] * conv_w[:, k] for k in range(K))) + conv_b
        hBC = jax.nn.silu(conv)
        h, Bm, Cm = jnp.split(hBC, [E, E + G * N], axis=-1)
        dt = jax.nn.softplus(dt + dt_bias)
        A = -jnp.exp(A_log)
        h = h.reshape(b, s, NH, P)
        Bm = jnp.tile(Bm.reshape(b, s, G, N), (1, 1, NH // G, 1))
        Cm = jnp.tile(Cm.reshape(b, s, G, N), (1, 1, NH // G, 1))
        pad = -s % CS
        D_res = D[:, None] * jnp.pad(h, ((0, 0), (0, pad), (0, 0), (0, 0)))
        h = h * dt[..., None]
        A_d = A * dt

        def chunk(t):
            t = jnp.pad(t, ((0, 0), (0, pad)) + ((0, 0),) * (t.ndim - 2))
            return t.reshape(b, -1, CS, *t.shape[2:])
        hc, Ac, Bc, Cc = (chunk(h), chunk(A_d), chunk(Bm), chunk(Cm))
        Ac = jnp.transpose(Ac, (0, 3, 1, 2))
        A_cs = jnp.cumsum(Ac, axis=-1)
        L = jnp.exp(segment_sum(Ac))
        Gm = jnp.einsum('bclhn,bcshn->bclsh', Cc, Bc)
        M = Gm * jnp.transpose(L, (0, 2, 3, 4, 1))
        Y_diag = jnp.einsum('bclsh,bcshp->bclhp', M, hc)
        decay = jnp.exp(A_cs[..., -1:] - A_cs)
        Bdec = Bc * jnp.transpose(decay, (0, 2, 3, 1))[..., None]
        states = jnp.einsum('bclhn,bclhp->bchpn', Bdec, hc)
        states = jnp.concatenate([jnp.zeros_like(states[:, :1]), states], axis=1)
        A_last = jnp.pad(A_cs[..., -1], ((0, 0), (0, 0), (1, 0)))
        dchunk = jnp.transpose(jnp.exp(segment_sum(A_last)), (0, 3, 2, 1))
        new_states = jnp.einsum('bzjh,bzhpn->bjhpn', dchunk, states)
        states = new_states[:, :-1]
        sdo = jnp.exp(A_cs)
        Y_off = jnp.einsum('bclhn,bchpn->bclhp', Cc, states) * jnp.transpose(sdo, (0, 2, 3, 1))[..., None]
        y = (Y_diag + Y_off).reshape(b, -1, NH, P) + D_res
        y = y[:, :s].reshape(b, s, E)
        yf = y * jax.nn.silu(gate)
        var = jnp.mean(yf * yf, axis=-1, keepdims=True)
        yn = norm_w * (yf * jax.lax.rsqrt(var + EPS))
        return yn @ out_proj_w.T

    def _L0_ffn_ref(x, router_w, router_bias, wg, wu, wd, swg, swu, swd):
        import jax, jax.numpy as jnp
        import numpy as np
        B, T, D = (2, 128, 256)
        E, F, K = (64, 64, 4)
        S, HS = (2, 64 * 4)
        b, t, d = x.shape
        flat = x.reshape(b * t, d)
        n = flat.shape[0]
        logits = flat @ router_w
        scores = jax.nn.softmax(logits, axis=-1)
        _, topk_idx = jax.lax.top_k(logits + router_bias, K)
        topk_scores = jnp.take_along_axis(scores, topk_idx, axis=-1)
        topk_scores = topk_scores / topk_scores.sum(axis=-1, keepdims=True)
        comb = jnp.zeros((n, E), dtype=flat.dtype).at[jnp.arange(n)[:, None], topk_idx].set(topk_scores)
        g = jax.nn.silu(jnp.einsum('nd,edf->nef', flat, wg))
        u = jnp.einsum('nd,edf->nef', flat, wu)
        routed = jnp.einsum('ne,nef,efd->nd', comb, g * u, wd)
        sg = jax.nn.silu(jnp.einsum('nd,sdh->nsh', flat, swg))
        su = jnp.einsum('nd,sdh->nsh', flat, swu)
        shared = jnp.einsum('nsh,shd->nd', sg * su, swd)
        return (routed + shared).reshape(b, t, d)
    x = L0_attn_x
    mod = (_silu(L0_c) @ L0_wmod).reshape(L0_c.shape[0], 6, 1, -1)
    sa, ca, ga, sb, cb, gb = (mod[:, 0], mod[:, 1], mod[:, 2], mod[:, 3], mod[:, 4], mod[:, 5])
    ga = (2 * (ga >= 0) - 1) * jnp.maximum(jnp.abs(ga), 0.25)
    gb = (2 * (gb >= 0) - 1) * jnp.maximum(jnp.abs(gb), 0.25)
    h = _layernorm(x, axis=-1) * (1 + ca) + sa
    x = x + ga * _L0_attn_ref(h, L0_attn_in_proj_w, L0_attn_conv_w, L0_attn_conv_b, L0_attn_dt_bias, L0_attn_A_log, L0_attn_D, L0_attn_norm_w, L0_attn_out_proj_w)
    h = _layernorm(x, axis=-1) * (1 + cb) + sb
    x = x + gb * _L0_ffn_ref(h, L0_ffn_router_w, L0_ffn_router_bias, L0_ffn_wg, L0_ffn_wu, L0_ffn_wd, L0_ffn_swg, L0_ffn_swu, L0_ffn_swd)
    return x

_drawn_inputs = setup_inputs


def setup_inputs(seed=0):
    import zlib

    import numpy as np

    out = dict(_drawn_inputs(seed))
    spreads = {'L0_attn_conv_b': (0.0, 0.1),
     'L0_attn_D': (1.0, 0.6),
     'L0_attn_norm_w': (1.0, 0.6),
     'L0_ffn_router_bias': (0.0, 0.8)}
    factors = {'L0_attn_conv_w': 3.574,
     'L0_attn_dt_bias': 37.409,
     'L0_attn_A_log': 8.0,
     'L0_ffn_router_w': 8.0,
     'L0_ffn_wg': 8.0,
     'L0_ffn_wu': 8.0,
     'L0_ffn_wd': 8.0,
     'L0_ffn_swg': 8.0,
     'L0_ffn_swu': 8.0,
     'L0_ffn_swd': 8.0}
    for name, (base, spread) in spreads.items():
        noise = np.random.default_rng([zlib.crc32(name.encode()), seed]).standard_normal(out[name].shape)
        drawn = base * np.exp(spread * noise) if base else spread * noise
        out[name] = jnp.asarray(drawn.astype(out[name].dtype))
    for name, factor in factors.items():
        out[name] = (out[name] * factor).astype(out[name].dtype)
    return out
```

```python
from contextlib import ExitStack

import concourse.bass as bass
from concourse import mybir

F32 = mybir.dt.float32
I32 = mybir.dt.int32
U32 = mybir.dt.uint32
ALU = mybir.AluOpType
ACT = mybir.ActivationFunctionType
AX = mybir.AxisListType

P = 128
S = 2048
H = 256
KH = H // P
EI = 512
KE = EI // P
NH, HP, N = 8, 64, 64
CONV = EI + 2 * N
CJ = CONV // P
TAPS = 4
PROJ = EI + CONV + NH
G2 = 2
GT = G2 * P
GROUPS = S // GT
TILES = S // P
NE, FF, TOP = 64, 64, 4
REGION = S + P
XT = 128
QT = 4
ROUNDS = XT // QT
SH = 512
KS = SH // P
LN_EPS = 1e-5
RMS_EPS = 1e-6
ARENA = 26500


class Event:
    def __init__(self, sem, per, ahead=1):
        self.sem, self.per, self.ahead = sem, per, ahead

    def at(self, g, k=None):
        return (g + self.ahead) * self.per + (self.per if k is None else k)


def bc(ap, axis, n):
    wide = ap.unsqueeze(axis)
    shape = list(wide.shape)
    shape[axis] = n
    return wide.broadcast_to(shape)


def build(nc, x, w_in, conv, rows8, norm_w, w_out, w_router, rbias, w_gu, w_d, w_sgu, w_sd, cvec, w_mod, out):
    with ExitStack() as ctx:
        def sb(name, shape, dt=F32):
            return ctx.enter_context(nc.sbuf_tensor(name, shape, dt))

        def sem(name):
            return ctx.enter_context(nc.semaphore(name))

        events = []

        def event(name, per):
            events.append(Event(sem(name), per))
            return events[-1]

        def dma_event(name, dmas=1):
            return Event(sem(name), 16 * dmas, ahead=0)

        expert_in = nc.dram_tensor("expert_in", (NE * REGION, H), F32).ap()
        expert_out = nc.dram_tensor("expert_out", (XT * P, H), F32).ap()

        bank = [ctx.enter_context(nc.psum_tensor(f"bank{b}", [P, 512], F32)) for b in (2, 3, 4, 5, 6, 7)]
        wide = ctx.enter_context(nc.psum_tensor("wide", [P, 1024], F32))
        B2, B3, B4, B5, B6, B7 = bank

        x_all = sb("x_all", [P, TILES, H])
        h2T_all = sb("h2T_all", [P, KH, S])
        gu = sb("gu", [P, NE * KH * P])
        ident = sb("ident", [P, P])
        ones = sb("ones", [P, P])
        gb_row = sb("gb_row", [P, H])
        idx_all = sb("idx_all", [P, TILES * TOP])
        rank_all = sb("rank_all", [P, TILES * TOP])
        cw_all = sb("cw_all", [P, TILES * TOP])
        run = sb("run", [P, NE])
        iota_e = sb("iota_e", [P, NE])
        neg_half = sb("neg_half", [P, 2])
        pidx = sb("pidx", [P, 1])

        arena = sb("arena", [P, ARENA])
        top = [0]

        def part(*shape, dt=F32, rows=P, of=arena, size=ARENA):
            n = 1
            for d in shape:
                n *= d
            assert top[0] + n <= size, (top[0], n)
            a = of[0:rows, top[0]:top[0] + n]
            top[0] += n + n % 2
            if dt != F32:
                a = a.bitcast(dt)
            if len(shape) == 2:
                a = a.rearrange("p (a b) -> p a b", b=shape[1])
            if len(shape) == 3:
                a = a.rearrange("p (a b c) -> p a b c", b=shape[1], c=shape[2])
            return a

        wi = part(KH, PROJ)
        wo = part(KE, H)
        wr = part(KH, NE)
        rb = part(NE)
        cvw = part(CJ, TAPS + 1)
        r8 = part(3, NH)
        nw = part(KE)
        tri = part(P)
        strict = part(P)
        before = part(P)
        iota8 = part(8, NE)
        cb_row = part(H)
        sb_row = part(H)
        ga_row = part(H)
        col1 = part(2 * KH)
        c_in = part(KH)
        c_silu = part(KH)
        neg_a = part(NH)
        st6 = part(G2, 6)
        mv1 = part(G2, 2)
        ve1 = part(2)
        rstd1 = part(2)
        z1 = part(G2, H)
        hT = part(KH, GT)
        cin = part(CJ, GT + TAPS - 1)
        acc = part(CJ, GT)
        xc = part(KE, GT)
        BT = part(GT, rows=N)
        CT = part(GT, rows=N)
        gs = part(G2, EI)
        dts = part(G2, NH)
        dtx = part(G2, NH)
        nab = part(G2, NH)
        lnp = part(G2, NH)
        dt = part(G2, NH)
        av = part(G2, NH)
        am = part(NH, P)
        ed = part(G2, 3 * NH)
        gb = part(G2, P + N)
        gm = part(G2, P)
        E = [part(NH, P) for _ in range(G2)]
        mod_at = top[0]
        xTs = part(G2, EI)
        xdt = part(G2, EI)
        xdd = part(G2, EI)
        xD = part(G2, EI)
        y = part(G2, EI)
        yT = part(G2, EI)
        state = part(EI, rows=N)
        junk = part(EI)
        ssq = part(2)
        vy = part(2)
        rstdy = part(2)
        x1 = part(G2, H)
        st6b = part(G2, 6)
        mv2 = part(G2, 2)
        ve2 = part(2)
        rstd2 = part(2)
        h2 = part(G2, H)
        h2T = part(KH, GT)
        lgs = part(G2, NE)
        lb = part(G2, NE)
        nm = part(2)
        el = part(G2, NE)
        m8 = part(G2, 8)
        ix8 = part(G2, 8, dt=U32)
        ixf = part(G2 * TOP)
        oh = part(G2 * TOP, NE)
        ohe = part(G2 * TOP, NE)
        ohr = part(G2 * TOP, NE)
        mask = part(G2, NE)
        cw = part(G2 * TOP)
        csum = part(2)
        rcs = part(2)
        rank = part(G2 * TOP)
        pos = part(G2 * TOP, dt=U32)
        wm = arena[:, mod_at:mod_at + KH * 6 * H].rearrange("p (k n) -> p k n", k=KH)

        top[0] = 0
        wd = part(NE * H, rows=FF)
        zeros = part(H)
        cnt = part(NE)
        cnt_i = part(NE, dt=I32)
        nt_i = part(NE, dt=I32)
        ntf = part(NE)
        one_e = part(NE)
        tend = part(NE)
        tstart = part(NE)
        le = part(NE)
        tab = part(8)
        fill_f = part(NE)
        fill_i = part(NE, dt=I32)
        tab_i = part(2 * XT, dt=I32)
        xsb = part(QT, H)
        xsT = part(KH, QT * P)
        sg = part(QT, FF)
        act = part(QT, FF)
        aT = part(QT * P, rows=FF)
        ysb = part(QT, H)
        selw = part(16, NE)
        selp = part(TILES * TOP)
        pos2 = part(TILES * TOP, dt=U32)
        wsh = part(KH, 2 * SH)
        wsd = part(KS, H)
        top[0] = 0
        third = {"of": gu, "size": NE * KH * P}
        shg = part(KS, GT, **third)
        hid = part(KS, GT, **third)
        yg = part(G2 * TOP, H, **third)
        comb = part(G2, H, **third)
        fin = part(G2, H, **third)

        s_x = sem("x_loaded")
        s_w = sem("weights_loaded")
        s_const = sem("constants_made")
        s_vec = sem("vector_setup")
        s_csilu = sem("c_silu_ready")
        s_modp = sem("mod_in_psum")
        s_mod = sem("mod_ready")
        s_gu = sem("gate_up_loaded")
        s_alone = sem("wait_alone")
        NW = 11

        stats1 = event("stats1", 2)
        mv1_ready = event("mv1_ready", 2)
        ve1_ready = event("ve1_ready", 1)
        rstd1_ready = event("rstd1_ready", 1)
        z1_ready = event("z1_ready", 2)
        z1T_done = event("z1T_done", 1)
        hT_ready = event("hT_ready", 2)
        convp_done = event("convp_done", 3)
        cin_ready = event("cin_ready", 3)
        dts_ready = event("dts_ready", 1)
        halo_saved = event("halo_saved", 1)
        tap_done = event("tap_done", CJ * TAPS)
        gatep_done = event("gatep_done", 2)
        xc_ready = event("xc_ready", 3)
        gs_ready = event("gs_ready", 2)
        dtx_ready = event("dtx_ready", 2)
        dte_ready = event("dte_ready", 2)
        dt_ready = event("dt_ready", 2)
        am_ready = event("am_ready", 2)
        sm_done = event("small_products_done", 2)
        gb_ready = event("gb_ready", 4)
        gm_ready = event("gm_ready", 2)
        seg_done = event("seg_done", 2)
        E_ready = event("E_ready", 2)
        M_ready = event("M_ready", 2)
        xT_done = event("xT_done", 2)
        xTs_ready = event("xTs_ready", 2)
        xdt_ready = event("xdt_ready", 2)
        xdd_ready = event("xdd_ready", 2)
        xD_ready = event("xD_ready", 2)
        yd_done = event("yd_done", 2)
        yo_done = event("yo_done", 2)
        sn_done = event("sn_done", 2)
        smul_done = event("state_scaled", 2)
        state_ready = event("state_ready", 2)
        y1_done = event("y1_done", 2)
        y2_done = event("y2_done", 2)
        y3_done = event("y3_done", 2)
        yf_done = event("yf_done", 2)
        ssq_ready = event("ssq_ready", 2)
        vy_ready = event("vy_ready", 2)
        rstdy_ready = event("rstdy_ready", 2)
        yT_done = event("yT_done", 2)
        yTs_ready = event("yTs_ready", 2)
        op_done = event("op_done", 2)
        att_done = event("att_done", 2)
        x1_ready = event("x1_ready", 2)
        stats2 = event("stats2", 2)
        mv2_ready = event("mv2_ready", 2)
        ve2_ready = event("ve2_ready", 1)
        rstd2_ready = event("rstd2_ready", 1)
        h2_step = event("h2_step", 4)
        h2_ready = event("h2_ready", 2)
        h2T_done = event("h2T_done", 1)
        h2T_ready = event("h2T_ready", 2)
        lg_done = event("lg_done", 1)
        lgs_ready = event("lgs_ready", 1)
        lb_ready = event("lb_ready", 1)
        nm_ready = event("nm_ready", 1)
        el_ready = event("el_ready", 2)
        m8_ready = event("m8_ready", 2)
        ix_ready = event("ix_ready", 2)
        ixf_ready = event("ixf_ready", 1)
        oh_ready = event("oh_ready", 1)
        mask_ready = event("mask_ready", 1)
        rank_done = event("rank_done", 1)
        ohr_ready = event("ohr_ready", 1)
        rank_ready = event("rank_ready", 1)
        pos_ready = event("pos_ready", 1)
        run_ready = event("run_ready", 2)
        scattered = dma_event("scattered", G2 * TOP)
        rows_free = event("scattered_rows_free", 1)
        cw_steps = event("cw_steps", 5)

        s_count = sem("counts_in_psum")
        s_plan = sem("plan_steps")
        s_tabp = sem("table_in_psum")
        s_tab = sem("table_ready")
        s_fill = sem("padding_filled")
        s_wd = sem("down_loaded")
        s_wsh = sem("shared_loaded")
        s_zero = sem("zeros_ready")
        xs_loaded = [dma_event(f"xs{q}_loaded") for q in range(QT)]
        xsp_done = event("xs_transposed", 1)
        xsT_ready = event("xsT_ready", 2)
        gup_done = event("gate_up_done", 1)
        sg_ready = event("sg_ready", 1)
        act_ready = event("act_ready", 1)
        aTp_done = event("act_transposed", 1)
        aT_ready = event("aT_ready", 1)
        down_done = event("down_done", 2)
        ys_ready = event("ys_ready", 2)
        ys_stored = dma_event("ys_stored")
        ys_free = event("ys_free", 1)
        s_sel = sem("gather_rows_steps")
        shp_done = event("shared_up_done", 2 * KS)
        shg_ready = event("shared_gate_ready", KS)
        hid_ready = event("hid_ready", KS)
        shd_done = event("shared_down_done", 2)
        comb_ready = event("comb_ready", 2 * (TOP + 1))
        fin_ready = event("fin_ready", 2)
        gathered = [dma_event(f"gathered{k}") for k in range(G2 * TOP)]
        stored = dma_event("stored")
        fin_free = event("fin_free", 1)

        block = ctx.enter_context(nc.Block())

        def wait(eng, ev, g, k=None):
            eng.wait_ge(ev.sem, ev.at(g, k))

        def wait_alone(eng, ev, g, k=None):
            eng.wait_ge(ev.sem, ev.at(g, k))
            eng.sem_inc(s_alone, 1)

        def tok(c):
            return slice(c * P, (c + 1) * P)

        @block.sync
        def _(sp):
            for ev in events:
                sp.sem_inc(ev.sem, ev.per)
            sp.dma_start(x_all[:], x.rearrange("(t p) d -> p t d", p=P)).then_inc(s_x, 16)
            sp.dma_start(c_in, cvec).then_inc(s_w, 16)
            sp.dma_start(wm, w_mod.rearrange("(k p) n -> p k n", p=P)).then_inc(s_w, 16)
            sp.dma_start(wi, w_in.rearrange("(k p) n -> p k n", p=P)).then_inc(s_w, 16)
            sp.dma_start(cvw, conv).then_inc(s_w, 16)
            sp.dma_start(r8, rows8).then_inc(s_w, 16)
            sp.dma_start(nw, norm_w).then_inc(s_w, 16)
            sp.dma_start(wo, w_out.rearrange("(k p) n -> p k n", p=P)).then_inc(s_w, 16)
            sp.dma_start(wr, w_router.rearrange("(k p) n -> p k n", p=P)).then_inc(s_w, 16)
            sp.dma_start(rb, rbias).then_inc(s_w, 16)
            sp.dma_start(gu[:], w_gu).then_inc(s_gu, 16)

            with sp.Fori(0, GROUPS) as g:
                wait(sp, scattered, g)
                sp.sem_inc(rows_free.sem, 1)

            L = GROUPS - 1
            wait(sp, scattered, L)
            wait(sp, cw_steps, L)
            wait(sp, pos_ready, L)
            sp.wait_ge(s_zero, 1)
            sp.wait_ge(s_plan, 1)
            sp.dma_start(wd, w_d).then_inc(s_wd, 16)
            sp.dma_start(wsh, w_sgu.rearrange("(k p) n -> p k n", p=P)).then_inc(s_wsh, 16)
            sp.dma_start(wsd, w_sd.rearrange("(k p) n -> p k n", p=P)).then_inc(s_wsh, 16)
            sp.wait_ge(s_tab, 1)
            with sp.Fori(0, NE) as e:
                row = sp.value_load(fill_i[0:1, bass.ds(e, 1)], min_val=0, max_val=NE * REGION - P)
                sp.dma_start(expert_in[bass.ds(row, P), :], zeros).then_inc(s_fill, 16)
            sp.wait_ge(s_fill, 16 * NE)
            sp.wait_ge(s_tab, 2)
            with sp.Fori(0, ROUNDS) as i:
                for q in range(QT):
                    row = sp.value_load(tab_i[0:1, bass.ds(i * QT + (XT + q), 1)], min_val=0, max_val=NE * REGION - P)
                    wait(sp, xsp_done, i - 1)
                    sp.dma_start(xsb[:, q, :], expert_in[bass.ds(row, P), :]).then_inc(xs_loaded[q].sem, 16)
            wait(sp, ys_stored, ROUNDS - 1)
            with sp.Fori(0, GROUPS) as g:
                wait(sp, fin_ready, g)
                sp.dma_start(out[bass.ds(g * GT, GT), :].rearrange("(c p) d -> p c d", p=P), fin).then_inc(stored.sem, 16)
                wait(sp, stored, g)
                sp.sem_inc(fin_free.sem, 1)
            wait(sp, stored, GROUPS - 1)

        @block.gpsimd
        def _(pool):
            pool_ = nc.gpsimd
            pool_.memset(ident[:], 0.0).then_inc(s_const, 1)
            pool_.memset(ones[:], 1.0).then_inc(s_const, 1)
            pool_.memset(run[:], 0.0).then_inc(s_const, 1)
            pool_.memset(neg_half[:], -0.5).then_inc(s_const, 1)
            pool_.iota(iota_e[:], [[1, NE]], base=0, channel_multiplier=0,
                       allow_small_or_imprecise_dtypes=True).then_inc(s_const, 1)
            pool_.iota(iota8, [[0, 8], [1, NE]], base=0, channel_multiplier=0,
                       allow_small_or_imprecise_dtypes=True).then_inc(s_const, 1)
            pool.wait_ge(s_const, 6)
            pool_.affine_select(out=ident[:], in_=ident[:], compare_op=ALU.not_equal, fill=1.0, base=0,
                                pattern=[[-1, P]], channel_multiplier=1).then_inc(s_const, 1)
            pool_.affine_select(out=tri, in_=ones[:], compare_op=ALU.is_ge, fill=0.0, base=0,
                                pattern=[[1, P]], channel_multiplier=-1).then_inc(s_const, 1)
            pool_.affine_select(out=strict, in_=ones[:], compare_op=ALU.is_gt, fill=0.0, base=0,
                                pattern=[[-1, P]], channel_multiplier=1).then_inc(s_const, 1)
            pool_.affine_select(out=before, in_=ones[:], compare_op=ALU.is_gt, fill=0.0, base=0,
                                pattern=[[1, P]], channel_multiplier=-1).then_inc(s_const, 1)
            pool_.iota(pidx[:], [[0, 1]], base=0, channel_multiplier=1,
                       allow_small_or_imprecise_dtypes=True).then_inc(s_const, 1)
            pool.wait_ge(s_const, 11)
            pool.wait_ge(s_w, 16 * (NW - 2))
            pool.wait_ge(s_modp, 8)
            pool.wait_ge(s_mod, 3)

            def rsqrt_front(f):
                wait(pool, ve1_ready, f)
                wait(pool, z1_ready, f - 1)
                pool_.tensor_tensor(rstd1, ve1, neg_half[:], ALU.pow).then_inc(rstd1_ready.sem, 1)

            def mix_inputs(g, c):
                wait(pool, dt_ready, g)
                if c:
                    wait(pool, seg_done, g, c)
                else:
                    wait(pool, seg_done, g - 1)
                pool_.tensor_tensor(am, bc(av[:, c, :], 2, P), bc(strict, 1, NH), ALU.mult).then_inc(am_ready.sem, 1)

            def mix_values(g, c):
                xs = xTs[:, c, :].rearrange("p (h d) -> p h d", d=HP)
                o = xdt[:, c, :].rearrange("p (h d) -> p h d", d=HP)
                wait(pool, xTs_ready, g, c + 1)
                wait(pool, yd_done, g - 1, c + 1)
                pool_.tensor_tensor(o, xs, bc(dt[:, c, :], 2, HP), ALU.mult).then_inc(xdt_ready.sem, 1)
                wait(pool, y3_done, g - 1, c + 1)
                pool_.tensor_tensor(xD[:, c, :].rearrange("p (h d) -> p h d", d=HP), xs, bc(r8[:, 2, :], 2, HP),
                                    ALU.mult).then_inc(xD_ready.sem, 1)
                wait(pool, xdt_ready, g, c + 1)
                wait(pool, gb_ready, g, 2 * c + 1)
                wait(pool, sn_done, g - 1, c + 1)
                pool_.tensor_tensor(xdd[:, c, :].rearrange("p (h d) -> p h d", d=HP), o, bc(ed[:, c, NH:2 * NH], 2, HP),
                                    ALU.mult).then_inc(xdd_ready.sem, 1)

            def gate(g, c):
                wait(pool, y2_done, g, c + 1)
                wait(pool, xD_ready, g, c + 1)
                pool_.tensor_tensor(y[:, c, :], y[:, c, :], xD[:, c, :], ALU.add).then_inc(y3_done.sem, 1)
                wait(pool, y3_done, g, c + 1)
                wait(pool, gs_ready, g, c + 1)
                pool_.tensor_tensor(y[:, c, :], y[:, c, :], gs[:, c, :], ALU.mult).then_inc(yf_done.sem, 1)

            def rsqrt_rms(g, c):
                wait(pool, vy_ready, g, c + 1)
                wait(pool, att_done, g - 1, c + 1)
                pool_.tensor_tensor(rstdy[:, c:c + 1], vy[:, c:c + 1], neg_half[:, 0:1], ALU.pow).then_inc(rstdy_ready.sem, 1)

            def rsqrt_route(g):
                wait(pool, ve2_ready, g)
                wait(pool, h2_step, g - 1)
                pool_.tensor_tensor(rstd2, ve2, neg_half[:], ALU.pow).then_inc(rstd2_ready.sem, 1)

            def scatter(g):
                wait(pool, rank_done, g)
                wait(pool, run_ready, g - 1)
                pool_.tensor_tensor(run[:], run[:], mask[:, 0, :], ALU.add).then_inc(run_ready.sem, 1)
                wait(pool, run_ready, g, 1)
                pool_.tensor_tensor(run[:], run[:], mask[:, 1, :], ALU.add).then_inc(run_ready.sem, 1)
                wait_alone(pool, pos_ready, g)
                wait_alone(pool, h2_ready, g)
                for c in range(G2):
                    for k in range(TOP):
                        j = c * TOP + k
                        pool_.indirect_dma_start(expert_in, bass.IndirectOffsetOnAxis(ap=pos[:, j:j + 1], axis=0),
                                                 h2[:, c, :], None).then_inc(scattered.sem, 16)

            def step(g, f):
                if g is not None:
                    mix_inputs(g, 0)
                if f is not None:
                    rsqrt_front(f)
                if g is None:
                    return
                mix_inputs(g, 1)
                mix_values(g, 0)
                mix_values(g, 1)
                gate(g, 0)
                gate(g, 1)
                rsqrt_rms(g, 0)
                rsqrt_rms(g, 1)
                rsqrt_route(g)
                scatter(g)

            step(None, 0)
            with pool.Fori(0, GROUPS - 1) as g:
                step(g, g + 1)
            step(GROUPS - 1, None)

            with pool.Fori(0, ROUNDS) as i:
                wait(pool, ys_stored, i)
                pool.sem_inc(ys_free.sem, 1)

            pool.wait_ge(s_sel, 13)
            wait(pool, ys_stored, ROUNDS - 1)
            for g in range(GROUPS):
                for c in range(G2):
                    for k in range(TOP):
                        j = c * TOP + k
                        at = (g * G2 + c) * TOP + k
                        if g:
                            wait(pool, comb_ready, g - 1, c * (TOP + 1) + k + 2)
                        pool_.indirect_dma_start(yg[:, j, :], None, expert_out,
                                                 bass.IndirectOffsetOnAxis(ap=pos2[:, at:at + 1], axis=0))\
                             .then_inc(gathered[j].sem, 16)

        @block.scalar
        def _(act_e):
            a = act_e
            sc = nc.scalar
            a.wait_ge(s_w, 16 * (NW - 2))
            sc.activation(c_silu, c_in, ACT.Silu).then_inc(s_csilu, 1)
            sc.activation(neg_a, r8[:, 1, :], ACT.Exp).then_inc(s_csilu, 1)
            a.wait_ge(s_vec, 2)

            def front_hT(f):
                wait(a, z1T_done, f)
                wait(a, gatep_done, f - 1)
                for k in range(KH):
                    sc.activation(hT[:, k, :], B6[:, k * GT:(k + 1) * GT], ACT.Identity, bias=col1[:, k:k + 1],
                                  scale=col1[:, KH + k:KH + k + 1]).then_inc(hT_ready.sem, 1)

            def front_conv_in(f):
                wait(a, halo_saved, f - 1)
                for n, b in enumerate((B7, B6)):
                    wait(a, convp_done, f, n + 1)
                    sc.activation(cin[:, 2 * n:2 * n + 2, TAPS - 1:], b[:, :].rearrange("p (j t) -> p j t", j=2),
                                  ACT.Copy).then_inc(cin_ready.sem, 1)
                wait(a, convp_done, f, 3)
                wait(a, dtx_ready, f - 1)
                sc.activation(cin[:, 4, TAPS - 1:], B7[:, 0:GT], ACT.Copy).then_inc(cin_ready.sem, 1)
                sc.activation(dts, B7[:, GT:GT + G2 * NH].rearrange("p (c h) -> p c h", c=G2), ACT.Copy)\
                  .then_inc(dts_ready.sem, 1)

            def front_silu(f):
                wait(a, yo_done, f - 1)
                wait(a, xT_done, f - 1)
                wait(a, tap_done, f)
                sc.activation(xc, acc[:, 0:KE, :], ACT.Silu).then_inc(xc_ready.sem, 1)
                sc.activation(BT, acc[0:N, KE, :], ACT.Silu).then_inc(xc_ready.sem, 1)
                sc.activation(CT, acc[N:P, KE, :], ACT.Silu).then_inc(xc_ready.sem, 1)
                for c, b in enumerate((B6, B7)):
                    wait(a, gatep_done, f, c + 1)
                    wait(a, yf_done, f - 1, c + 1)
                    sc.activation(gs[:, c, :], b[:, :], ACT.Silu).then_inc(gs_ready.sem, 1)

            def front_dt(f):
                wait(a, dtx_ready, f)
                sc.activation(lnp, nab, ACT.Exp).then_inc(dte_ready.sem, 1)
                wait(a, dte_ready, f, 1)
                sc.activation(lnp, lnp, ACT.Ln, bias=1.0).then_inc(dte_ready.sem, 1)

            def mix_small(g, c):
                wait(a, sm_done, g, c + 1)
                wait(a, y1_done, g - 1, c + 1)
                wait(a, smul_done, g - 1, c + 1)
                wait(a, xdd_ready, g - 1, c + 1)
                sc.activation(ed[:, c, :], B2[:, 0:3 * NH], ACT.Exp).then_inc(gb_ready.sem, 1)
                wait(a, gm_ready, g - 1, c + 1)
                wait(a, sn_done, g - 1, c + 1)
                sc.activation(gb[:, c, :], B2[:, P:2 * P + N], ACT.Copy).then_inc(gb_ready.sem, 1)

            def mix_xT(g, c):
                wait(a, xT_done, g, c + 1)
                wait(a, xD_ready, g - 1, c + 1)
                sc.activation(xTs[:, c, :], B3[:, :], ACT.Copy).then_inc(xTs_ready.sem, 1)

            def mix_E(g, c):
                wait(a, seg_done, g, c + 1)
                wait(a, yd_done, g - 1, c + 1)
                sc.activation(E[c], wide[:, :].rearrange("p (h l) -> p h l", l=P), ACT.Exp).then_inc(E_ready.sem, 1)

            def mix_square(g, c):
                wait(a, yf_done, g, c + 1)
                wait(a, vy_ready, g - 1, c + 1)
                if c:
                    wait(a, ssq_ready, g, c)
                else:
                    wait(a, ssq_ready, g - 1)
                sc.activation(junk, y[:, c, :], ACT.Square, accum_out=ssq[:, c:c + 1]).then_inc(ssq_ready.sem, 1)

            def mix_yT(g, c):
                wait(a, yT_done, g, c + 1)
                wait(a, op_done, g - 1, c + 1)
                sc.activation(yT[:, c, :], B3[:, :], ACT.Copy).then_inc(yTs_ready.sem, 1)

            def route_h2T(g):
                wait(a, lg_done, g - 1)
                wait(a, h2T_done, g)
                sc.activation(h2T, B3[:, :].rearrange("p (k t) -> p k t", k=KH), ACT.Copy).then_inc(h2T_ready.sem, 1)
                sc.activation(h2T_all[:, :, bass.ds(g * GT, GT)], B3[:, :].rearrange("p (k t) -> p k t", k=KH),
                              ACT.Copy).then_inc(h2T_ready.sem, 1)

            def route_exp(g):
                wait(a, nm_ready, g)
                wait(a, cw_steps, g - 1)
                for c in range(G2):
                    sc.activation(el[:, c, :], lgs[:, c, :], ACT.Exp, bias=nm[:, c:c + 1]).then_inc(el_ready.sem, 1)

            def step(g, f):
                if g is not None:
                    mix_small(g, 0)
                    mix_xT(g, 0)
                    mix_E(g, 0)
                    mix_small(g, 1)
                    mix_xT(g, 1)
                    mix_E(g, 1)
                if f is not None:
                    front_hT(f)
                    front_conv_in(f)
                if g is not None:
                    for c in range(G2):
                        mix_square(g, c)
                        mix_yT(g, c)
                if f is not None:
                    front_silu(f)
                    front_dt(f)
                if g is not None:
                    route_h2T(g)
                    route_exp(g)

            step(None, 0)
            with a.Fori(0, GROUPS - 1) as g:
                step(g, g + 1)
            step(GROUPS - 1, None)

            def x_copy(i):
                wait(a, xsp_done, i)
                wait(a, gup_done, i - 1)
                sc.activation(xsT[:, 0, :], wide[:, 0:QT * P], ACT.Copy).then_inc(xsT_ready.sem, 1)

            def store(i):
                wait(a, ys_ready, i)
                a.dma_start(expert_out[bass.ds(i * (QT * P), QT * P), :].rearrange("(q p) d -> p q d", p=P), ysb)\
                 .then_inc(ys_stored.sem, 16)

            def down_copy(i):
                wait(a, down_done, i, 1)
                wait(a, ys_free, i - 1)
                sc.activation(ysb[:, 0:2, :], B4[:, :].rearrange("p (q d) -> p q d", q=2), ACT.Copy).then_inc(ys_ready.sem, 1)

            x_copy(0)
            with a.Fori(0, ROUNDS) as i:
                wait(a, gup_done, i)
                wait(a, act_ready, i - 1)
                sc.activation(sg, B2[:, :].rearrange("p (q f) -> p q f", q=QT)[:, :, 0:FF], ACT.Silu).then_inc(sg_ready.sem, 1)
                x_copy(i + 1)
                down_copy(i)
                store(i)

            with a.Fori(0, GROUPS) as g:
                for j in range(KS):
                    wait(a, shp_done, g, 2 * j + 1)
                    wait(a, hid_ready, g - 1, j + 1)
                    sc.activation(shg[:, j, :], (B2, B4)[j % 2][:, 0:GT], ACT.Silu).then_inc(shg_ready.sem, 1)

        @block.tensor
        def _(pe):
            te = nc.tensor

            pe.wait_ge(s_csilu, 1)
            pe.wait_ge(s_const, 10)
            for n in range(2 * KH):
                for k in range(KH):
                    mm = te.matmul(B2[:, n:n + 1], wm[:, k, n * P:(n + 1) * P], c_silu[:, k:k + 1],
                                   start=(k == 0), stop=(k == KH - 1))
            mm.then_inc(s_modp, 4)
            for n, b in ((2, B4), (3, B5), (4, B6), (5, B7)):
                for k in range(KH):
                    mm = te.matmul(b[:, 0:H], c_silu[:, k:k + 1].broadcast_to([P, P]), wm[:, k, n * H:(n + 1) * H],
                                   start=(k == 0), stop=(k == KH - 1))
                mm.then_inc(s_modp, 1)
            pe.wait_ge(s_mod, 6)

            def front_zT(f):
                wait(pe, z1_ready, f)
                wait(pe, gs_ready, f - 1)
                for k in range(KH):
                    for c in range(G2):
                        mm = te.transpose(B6[:, k * GT + c * P:k * GT + (c + 1) * P], z1[:, c, k * P:(k + 1) * P], ident[:])
                mm.then_inc(z1T_done.sem, 1)

            def front_conv(f):
                wait(pe, hT_ready, f)
                for n, b in enumerate((B7, B6, B7)):
                    if n == 2:
                        wait(pe, cin_ready, f, 1)
                    for j in range(2 * n, min(2 * n + 2, CJ)):
                        for k in range(KH):
                            mm = te.matmul(b[:, (j % 2) * GT:(j % 2 + 1) * GT], wi[:, k, EI + j * P:EI + (j + 1) * P],
                                           hT[:, k, :], start=(k == 0), stop=(k == KH - 1))
                    if n < 2:
                        mm.then_inc(convp_done.sem, 1)
                for c in range(G2):
                    for k in range(KH):
                        mm = te.matmul(B7[:, GT + c * NH:GT + (c + 1) * NH], hT[:, k, tok(c)], wi[:, k, PROJ - NH:PROJ],
                                       start=(k == 0), stop=(k == KH - 1))
                mm.then_inc(convp_done.sem, 1)

            def front_gate(f, c):
                wait(pe, cin_ready, f, 2 + c)
                if c:
                    wait(pe, dts_ready, f)
                for k in range(KH):
                    mm = te.matmul((B6, B7)[c][:, :], hT[:, k, tok(c)], wi[:, k, 0:EI], start=(k == 0), stop=(k == KH - 1))
                mm.then_inc(gatep_done.sem, 1)

            def mix_small(g, c):
                wait(pe, dt_ready, g)
                wait(pe, xc_ready, g)
                if c:
                    wait(pe, gb_ready, g, 2 * c)
                else:
                    wait(pe, gb_ready, g - 1)
                for n, m in enumerate((tri, strict, ones[:])):
                    te.matmul(B2[:, n * NH:(n + 1) * NH], m, av[:, c, :], start=True, stop=True)
                te.matmul(B2[:, P:2 * P], BT[:, tok(c)], CT[:, tok(c)], start=True, stop=True)
                te.transpose(B2[:, 2 * P:2 * P + N], BT[:, tok(c)], ident[0:N, 0:N]).then_inc(sm_done.sem, 1)

            def mix_xT(g, c):
                if c:
                    wait(pe, xTs_ready, g, c)
                else:
                    wait(pe, h2T_ready, g - 1)
                for j in range(KE):
                    mm = te.transpose(B3[:, j * P:(j + 1) * P], xc[:, j, tok(c)], ident[:])
                mm.then_inc(xT_done.sem, 1)

            def mix_seg(g, c):
                wait(pe, am_ready, g, c + 1)
                if c:
                    wait(pe, E_ready, g, c)
                else:
                    wait(pe, E_ready, g - 1)
                for h in range(NH):
                    mm = te.matmul(wide[:, h * P:(h + 1) * P], am[:, h, :], tri, start=True, stop=True)
                mm.then_inc(seg_done.sem, 1)

            def mix_y(g, c):
                wait(pe, M_ready, g, c + 1)
                wait(pe, xdt_ready, g, c + 1)
                if c:
                    wait(pe, y2_done, g, c)
                    wait(pe, y1_done, g, c)
                else:
                    wait(pe, lgs_ready, g - 1)
                    wait(pe, ohr_ready, g - 1)
                for h in range(NH):
                    mm = te.matmul(B4[:, h * HP:(h + 1) * HP], E[c][:, h, :], xdt[:, c, h * HP:(h + 1) * HP],
                                   start=True, stop=True)
                mm.then_inc(yd_done.sem, 1)
                if c:
                    wait(pe, state_ready, g, c)
                else:
                    wait(pe, state_ready, g - 1)
                te.matmul(B5[:, :], CT[:, tok(c)], state, start=True, stop=True).then_inc(yo_done.sem, 1)
                wait(pe, xdd_ready, g, c + 1)
                if not c:
                    wait(pe, xTs_ready, g)
                te.matmul(B3[0:N, :], gb[:, c, P:P + N], xdd[:, c, :], start=True, stop=True).then_inc(sn_done.sem, 1)

            def mix_yT(g, c):
                wait(pe, yf_done, g, c + 1)
                if c:
                    wait(pe, yTs_ready, g, c)
                else:
                    wait(pe, state_ready, g)
                for j in range(KE):
                    mm = te.transpose(B3[:, j * P:(j + 1) * P], y[:, c, j * P:(j + 1) * P], ident[:])
                mm.then_inc(yT_done.sem, 1)

            def mix_out(g, c):
                wait(pe, yTs_ready, g, c + 1)
                if c:
                    wait(pe, att_done, g, c)
                else:
                    wait(pe, y2_done, g)
                for j in range(KE):
                    mm = te.matmul(B4[:, 0:H], yT[:, c, j * P:(j + 1) * P], wo[:, j, :], start=(j == 0), stop=(j == KE - 1))
                mm.then_inc(op_done.sem, 1)

            def route(g):
                wait(pe, h2_ready, g)
                wait(pe, yTs_ready, g)
                for k in range(KH):
                    for c in range(G2):
                        mm = te.transpose(B3[:, k * GT + c * P:k * GT + (c + 1) * P], h2[:, c, k * P:(k + 1) * P], ident[:])
                mm.then_inc(h2T_done.sem, 1)
                wait(pe, h2T_ready, g, 1)
                wait(pe, att_done, g)
                for c in range(G2):
                    for k in range(KH):
                        mm = te.matmul(B4[:, c * NE:(c + 1) * NE], h2T[:, k, tok(c)], wr[:, k, :],
                                       start=(k == 0), stop=(k == KH - 1))
                mm.then_inc(lg_done.sem, 1)
                wait(pe, mask_ready, g)
                wait(pe, run_ready, g - 1)
                wait(pe, y1_done, g)
                te.matmul(B5[:, 0:NE], before, mask[:, 0, :], start=True, stop=False)
                te.matmul(B5[:, 0:NE], ones[:], run[:], start=False, stop=True)
                te.matmul(B5[:, NE:2 * NE], before, mask[:, 1, :], start=True, stop=False)
                te.matmul(B5[:, NE:2 * NE], ones[:], mask[:, 0, :], start=False, stop=False)
                te.matmul(B5[:, NE:2 * NE], ones[:], run[:], start=False, stop=True).then_inc(rank_done.sem, 1)

            def step(g, f):
                if g is not None:
                    for c in range(G2):
                        mix_small(g, c)
                        mix_xT(g, c)
                        mix_seg(g, c)
                if f is not None:
                    front_zT(f)
                if g is not None:
                    mix_y(g, 0)
                if f is not None:
                    front_conv(f)
                if g is not None:
                    mix_y(g, 1)
                    mix_yT(g, 0)
                if f is not None:
                    front_gate(f, 0)
                if g is not None:
                    mix_out(g, 0)
                    mix_yT(g, 1)
                if f is not None:
                    front_gate(f, 1)
                if g is not None:
                    mix_out(g, 1)
                    route(g)

            step(None, 0)
            with pe.Fori(0, GROUPS - 1) as g:
                step(g, g + 1)
            step(GROUPS - 1, None)

            wait(pe, run_ready, GROUPS - 1)
            wait(pe, ohr_ready, GROUPS - 1)
            te.matmul(B5[:, 0:NE], ones[:], run[:], start=True, stop=True).then_inc(s_count, 1)
            pe.wait_ge(s_plan, 15)
            te.matmul(B5[0:1, 0:XT], tab[:, 0:1], ident[:], start=True, stop=True)
            te.matmul(B5[0:1, XT:2 * XT], tab[:, 1:2], ident[:], start=True, stop=True).then_inc(s_tabp, 1)

            def x_turn(i):
                for q in range(QT):
                    wait(pe, xs_loaded[q], i)
                wait(pe, xsT_ready, i - 1)
                for q in range(QT):
                    for k in range(KH):
                        mm = te.transpose(wide[:, (k * QT + q) * P:(k * QT + q + 1) * P], xsb[:, q, k * P:(k + 1) * P], ident[:])
                mm.then_inc(xsp_done.sem, 1)

            def up(i):
                offs = [pe.value_load(tab_i[0:1, bass.ds(i * QT + q, 1)], min_val=0, max_val=(NE - 1) * H) for q in range(QT)]
                wait(pe, xsT_ready, i)
                wait(pe, act_ready, i - 1)
                for q in range(QT):
                    for k in range(KH):
                        mm = te.matmul(B2[:, q * P:(q + 1) * P], xsT[:, k, q * P:(q + 1) * P],
                                       gu[:, bass.ds(offs[q] + k * P, P)], start=(k == 0), stop=(k == KH - 1))
                mm.then_inc(gup_done.sem, 1)
                return offs

            def down(i, offs):
                wait(pe, aT_ready, i)
                wait(pe, ys_ready, i - 1)
                for q in range(QT):
                    mm = te.matmul((B4, B5)[q // 2][:, (q % 2) * H:(q % 2 + 1) * H], aT[:, q * P:(q + 1) * P],
                                   wd[0:FF, bass.ds(offs[q], H)], start=True, stop=True)
                    if q % 2:
                        mm.then_inc(down_done.sem, 1)

            def act_turn(i):
                wait_alone(pe, act_ready, i)
                wait_alone(pe, aT_ready, i - 1)
                for q in range(QT):
                    mm = te.transpose(B3[0:FF, q * P:(q + 1) * P], act[:, q, :], ident[:])
                mm.then_inc(aTp_done.sem, 1)

            pe.wait_ge(s_gu, 16)
            pe.wait_ge(s_wd, 16)
            pe.wait_ge(s_tab, 2)
            x_turn(0)
            with pe.Fori(0, ROUNDS - 1) as i:
                offs = up(i)
                x_turn(i + 1)
                act_turn(i)
                down(i, offs)
            offs = up(ROUNDS - 1)
            wait(pe, xsT_ready, ROUNDS - 1)
            te.transpose(wide[:, 0:P], ones[:], ident[:])
            te.transpose(wide[:, QT * P:(QT + 1) * P], ones[:], ident[:]).then_inc(xsp_done.sem, 1)
            act_turn(ROUNDS - 1)
            down(ROUNDS - 1, offs)

            pe.wait_ge(s_wsh, 32)
            wait(pe, ys_ready, ROUNDS - 1)
            with pe.Fori(0, GROUPS) as g:
                for j in range(KS):
                    for u in range(2):
                        b = ((B2, B4), (B3, B5))[u][j % 2]
                        if j >= 2:
                            wait(pe, hid_ready, g, j - 1)
                        else:
                            wait(pe, hid_ready, g - 1, KS - 1 + j)
                        for k in range(KH):
                            mm = te.matmul(b[:, 0:GT], wsh[:, k, u * SH + j * P:u * SH + (j + 1) * P],
                                           h2T_all[:, k, bass.ds(g * GT, GT)], start=(k == 0), stop=(k == KH - 1))
                        mm.then_inc(shp_done.sem, 1)
                wait(pe, hid_ready, g)
                for c in range(G2):
                    wait(pe, comb_ready, g - 1, c * (TOP + 1) + 1)
                    for j in range(KS):
                        mm = te.matmul((B6, B7)[c][:, 0:H], hid[:, j, tok(c)], wsd[:, j, :], start=(j == 0), stop=(j == KS - 1))
                    mm.then_inc(shd_done.sem, 1)

        @block.vector
        def _(dve):
            ve = nc.vector
            halo = cin[:, :, 0:TAPS - 1]
            ve.memset(state, 0.0).then_inc(s_vec, 1)
            ve.memset(halo, 0.0).then_inc(s_vec, 1)
            dve.wait_ge(s_csilu, 2)
            ve.tensor_scalar(neg_a, neg_a, -1.0, None, ALU.mult).then_inc(s_mod, 1)
            dve.wait_ge(s_modp, 8)
            ve.tensor_copy(col1[:, 0:KH], B2[:, 0:KH]).then_inc(s_mod, 1)
            ve.tensor_scalar(col1[:, KH:2 * KH], B2[:, KH:2 * KH], 1.0, None, ALU.add).then_inc(s_mod, 1)
            ve.tensor_copy(sb_row, B5[:, 0:H]).then_inc(s_mod, 1)
            ve.tensor_scalar(cb_row, B6[:, 0:H], 1.0, None, ALU.add).then_inc(s_mod, 1)
            for n, (b, row, tmp) in enumerate(((B4, ga_row, z1[:, 0, :]), (B7, gb_row[:], z1[:, 1, :]))):
                v = 2 + 4 * n
                ve.tensor_copy(tmp, b[:, 0:H]).then_inc(s_vec, 1)
                dve.wait_ge(s_vec, v + 1)
                ve.scalar_tensor_tensor(out=row, in0=tmp, scalar=-1.0, in1=tmp, op0=ALU.mult, op1=ALU.max).then_inc(s_vec, 1)
                dve.wait_ge(s_vec, v + 2)
                ve.tensor_scalar(row, row, 0.25, None, ALU.max).then_inc(s_vec, 1)
                ve.tensor_scalar(tmp, tmp, 0.0, 2.0, ALU.is_ge, ALU.mult).then_inc(s_vec, 1)
                dve.wait_ge(s_vec, v + 4)
                ins = ve.scalar_tensor_tensor(out=row, in0=tmp, scalar=-1.0, in1=row, op0=ALU.add, op1=ALU.mult)
                ins.then_inc(s_mod, 1)
            dve.wait_ge(s_w, 16 * (NW - 2))
            for j in range(KE):
                ve.tensor_scalar(wo[:, j, :], wo[:, j, :], nw[:, j:j + 1], None, ALU.mult).then_inc(s_mod, 1)
            dve.wait_ge(s_const, 10)
            dve.wait_ge(s_mod, 11)
            dve.wait_ge(s_x, 16)

            def front_stats(f):
                for c in range(G2):
                    ve.bn_stats(st6[:, c, :], x_all[:, f * G2 + c, :]).then_inc(stats1.sem, 1)
                for c in range(G2):
                    wait_alone(dve, stats1, f, c + 1)
                    ve.bn_aggr(mv1[:, c, :], st6[:, c, :]).then_inc(mv1_ready.sem, 1)
                wait(dve, mv1_ready, f)
                wait(dve, rstd1_ready, f - 1)
                ve.tensor_scalar(ve1, mv1[:, :, 1], LN_EPS, None, ALU.add).then_inc(ve1_ready.sem, 1)

            def front_z(f):
                wait(dve, rstd1_ready, f)
                wait(dve, z1T_done, f - 1)
                for c in range(G2):
                    ve.tensor_scalar(z1[:, c, :], x_all[:, f * G2 + c, :], mv1[:, c, 0:1], rstd1[:, c:c + 1],
                                     ALU.subtract, ALU.mult).then_inc(z1_ready.sem, 1)

            def front_conv(f, js, wait_acc):
                for j in js:
                    wait(dve, cin_ready, f, j // 2 + 1)
                    if wait_acc:
                        wait(dve, xc_ready, f - 1)
                    ve.tensor_scalar(acc[:, j, :], cin[:, j, 0:GT], cvw[:, j, 0:1], cvw[:, j, TAPS:TAPS + 1],
                                     ALU.mult, ALU.add).then_inc(tap_done.sem, 1)
                for k in range(1, TAPS):
                    for n, j in enumerate(js):
                        wait(dve, tap_done, f, js[0] * TAPS + (k - 1) * len(js) + n + 1)
                        ve.scalar_tensor_tensor(out=acc[:, j, :], in0=cin[:, j, k:k + GT], scalar=cvw[:, j, k:k + 1],
                                                in1=acc[:, j, :], op0=ALU.mult, op1=ALU.add).then_inc(tap_done.sem, 1)

            def front_halo(f):
                wait(dve, tap_done, f)
                ve.tensor_copy(halo, cin[:, :, GT:]).then_inc(halo_saved.sem, 1)

            def front_dtx(f):
                wait(dve, dts_ready, f)
                wait(dve, dt_ready, f - 1)
                ve.tensor_tensor(dtx, dts, bc(r8[:, 0, :], 1, G2), ALU.add).then_inc(dtx_ready.sem, 1)
                wait(dve, dtx_ready, f, 1)
                wait(dve, dte_ready, f - 1)
                ve.scalar_tensor_tensor(out=nab, in0=dtx, scalar=-1.0, in1=dtx, op0=ALU.mult, op1=ALU.min).then_inc(dtx_ready.sem, 1)

            def front_dt(f):
                wait(dve, dte_ready, f)
                wait(dve, xdt_ready, f - 1)
                ve.scalar_tensor_tensor(out=dt, in0=dtx, scalar=0.0, in1=lnp, op0=ALU.max, op1=ALU.add)\
                  .then_inc(dt_ready.sem, 1)
                wait(dve, dt_ready, f, 1)
                wait(dve, am_ready, f - 1)
                wait(dve, sm_done, f - 1)
                ve.tensor_tensor(av, dt, bc(neg_a, 1, G2), ALU.mult).then_inc(dt_ready.sem, 1)

            def mix_M(g, c):
                wait(dve, gb_ready, g, 2 * c + 2)
                ve.tensor_tensor(gm[:, c, :], gb[:, c, 0:P], tri, ALU.mult).then_inc(gm_ready.sem, 1)
                wait(dve, gm_ready, g, c + 1)
                wait(dve, E_ready, g, c + 1)
                ve.tensor_tensor(E[c], E[c], bc(gm[:, c, :], 1, NH), ALU.mult).then_inc(M_ready.sem, 1)

            def mix_y(g, c):
                heads = lambda ap: ap.rearrange("p (h d) -> p h d", d=HP)
                wait(dve, yo_done, g, c + 1)
                wait(dve, yT_done, g - 1, c + 1)
                wait(dve, ssq_ready, g - 1, c + 1)
                ve.tensor_tensor(heads(y[:, c, :]), heads(B5[:, :]), bc(ed[:, c, 0:NH], 2, HP), ALU.mult)\
                  .then_inc(y1_done.sem, 1)
                ve.tensor_tensor(heads(state), heads(state), bc(ed[0:N, c, 2 * NH:], 2, HP), ALU.mult)\
                  .then_inc(smul_done.sem, 1)
                wait(dve, y1_done, g, c + 1)
                ve.tensor_tensor(y[:, c, :], y[:, c, :], B4[:, :], ALU.add).then_inc(y2_done.sem, 1)
                wait(dve, smul_done, g, c + 1)
                wait(dve, sn_done, g, c + 1)
                ve.tensor_tensor(state, state, B3[0:N, :], ALU.add).then_inc(state_ready.sem, 1)

            def mix_rms(g, c):
                wait(dve, ssq_ready, g, c + 1)
                wait(dve, rstdy_ready, g - 1, c + 1)
                ve.tensor_scalar(vy[:, c:c + 1], ssq[:, c:c + 1], 1.0 / EI, RMS_EPS, ALU.mult, ALU.add)\
                  .then_inc(vy_ready.sem, 1)

            def mix_residual(g, c):
                wait(dve, op_done, g, c + 1)
                wait(dve, rstdy_ready, g, c + 1)
                ve.scalar_tensor_tensor(out=x1[:, c, :], in0=B4[:, 0:H], scalar=rstdy[:, c:c + 1], in1=ga_row,
                                        op0=ALU.mult, op1=ALU.mult).then_inc(att_done.sem, 1)
                wait(dve, att_done, g, c + 1)
                ve.tensor_tensor(x1[:, c, :], x1[:, c, :], x_all[:, g * G2 + c, :], ALU.add).then_inc(x1_ready.sem, 1)

            def route_norm(g):
                for c in range(G2):
                    wait(dve, x1_ready, g, c + 1)
                    ve.bn_stats(st6b[:, c, :], x1[:, c, :]).then_inc(stats2.sem, 1)
                    ve.tensor_copy(x_all[:, g * G2 + c, :], x1[:, c, :])
                for c in range(G2):
                    wait_alone(dve, stats2, g, c + 1)
                    ve.bn_aggr(mv2[:, c, :], st6b[:, c, :]).then_inc(mv2_ready.sem, 1)
                wait(dve, mv2_ready, g)
                wait(dve, rstd2_ready, g - 1)
                ve.tensor_scalar(ve2, mv2[:, :, 1], LN_EPS, None, ALU.add).then_inc(ve2_ready.sem, 1)
                wait(dve, rstd2_ready, g)
                wait(dve, rows_free, g - 1)
                wait(dve, h2T_done, g - 1)
                for c in range(G2):
                    ve.tensor_scalar(h2[:, c, :], x1[:, c, :], mv2[:, c, 0:1], rstd2[:, c:c + 1],
                                     ALU.subtract, ALU.mult).then_inc(h2_step.sem, 1)
                for c in range(G2):
                    wait(dve, h2_step, g, c + 1)
                    ve.tensor_tensor(h2[:, c, :], h2[:, c, :], cb_row, ALU.mult).then_inc(h2_step.sem, 1)
                for c in range(G2):
                    wait(dve, h2_step, g, c + 3)
                    ve.tensor_tensor(h2[:, c, :], h2[:, c, :], sb_row, ALU.add).then_inc(h2_ready.sem, 1)

            def route(g):
                wait(dve, lg_done, g)
                wait(dve, el_ready, g - 1)
                ve.tensor_copy(lgs, B4[:, 0:G2 * NE].rearrange("p (c e) -> p c e", c=G2)).then_inc(lgs_ready.sem, 1)
                wait(dve, lgs_ready, g)
                ve.tensor_tensor(lb, lgs, bc(rb, 1, G2), ALU.add).then_inc(lb_ready.sem, 1)
                ve.tensor_reduce(nm, lgs, AX.X, ALU.max, negate=True).then_inc(nm_ready.sem, 1)
                wait_alone(dve, lb_ready, g)
                for c in range(G2):
                    ve.max(m8[:, c, :], lb[:, c, :]).then_inc(m8_ready.sem, 1)
                for c in range(G2):
                    wait_alone(dve, m8_ready, g, c + 1)
                    ve.max_index(ix8[:, c, :], m8[:, c, :], lb[:, c, :]).then_inc(ix_ready.sem, 1)
                wait(dve, ix_ready, g)
                four = lambda ap: ap.rearrange("p (c k) -> p c k", c=G2)
                ve.tensor_copy(four(ixf), ix8[:, :, 0:TOP]).then_inc(ixf_ready.sem, 1)
                wait(dve, ixf_ready, g)
                ve.tensor_tensor(oh, iota8, bc(ixf, 2, NE), ALU.is_equal).then_inc(oh_ready.sem, 1)
                ve.tensor_copy(idx_all[:, bass.ds(g * (G2 * TOP), G2 * TOP)], ixf)
                wait(dve, oh_ready, g)
                wait(dve, run_ready, g - 1)
                ve.tensor_reduce(mask, oh.rearrange("p (c k) e -> p c e k", c=G2), AX.X, ALU.add).then_inc(mask_ready.sem, 1)
                wait(dve, el_ready, g)
                o4 = lambda ap: ap.rearrange("p (c k) e -> p c k e", c=G2)
                ve.tensor_tensor(o4(ohe), o4(oh), bc(el, 2, TOP), ALU.mult).then_inc(cw_steps.sem, 1)
                wait(dve, cw_steps, g, 1)
                ve.tensor_reduce(cw, ohe, AX.X, ALU.add).then_inc(cw_steps.sem, 1)
                wait(dve, cw_steps, g, 2)
                ve.tensor_reduce(csum, four(cw), AX.X, ALU.add).then_inc(cw_steps.sem, 1)
                wait(dve, cw_steps, g, 3)
                ve.reciprocal(rcs, csum).then_inc(cw_steps.sem, 1)
                wait(dve, cw_steps, g, 4)
                ve.tensor_tensor(four(cw_all[:, bass.ds(g * (G2 * TOP), G2 * TOP)]), four(cw), bc(rcs, 2, TOP), ALU.mult)\
                  .then_inc(cw_steps.sem, 1)
                wait(dve, rank_done, g)
                ve.tensor_tensor(o4(ohr), o4(oh), bc(B5[:, 0:G2 * NE].rearrange("p (c e) -> p c e", c=G2), 2, TOP), ALU.mult)\
                  .then_inc(ohr_ready.sem, 1)
                wait(dve, ohr_ready, g)
                ve.tensor_reduce(rank, ohr, AX.X, ALU.add).then_inc(rank_ready.sem, 1)
                wait(dve, rank_ready, g)
                wait(dve, rows_free, g - 1)
                ve.scalar_tensor_tensor(out=pos, in0=ixf, scalar=float(REGION), in1=rank, op0=ALU.mult, op1=ALU.add)\
                  .then_inc(pos_ready.sem, 1)
                ve.tensor_copy(rank_all[:, bass.ds(g * (G2 * TOP), G2 * TOP)], rank)

            def step(g, f):
                if f is not None:
                    front_stats(f)
                if g is not None:
                    mix_M(g, 0)
                if f is not None:
                    front_z(f)
                if g is not None:
                    mix_M(g, 1)
                    mix_y(g, 0)
                if f is not None:
                    front_conv(f, (0, 1), True)
                if g is not None:
                    mix_y(g, 1)
                if f is not None:
                    front_conv(f, (2, 3), False)
                    front_conv(f, (4,), False)
                    front_halo(f)
                    front_dtx(f)
                if g is not None:
                    for c in range(G2):
                        mix_rms(g, c)
                        mix_residual(g, c)
                if f is not None:
                    front_dt(f)
                if g is not None:
                    route_norm(g)
                    route(g)

            step(None, 0)
            with dve.Fori(0, GROUPS - 1) as g:
                step(g, g + 1)
            step(GROUPS - 1, None)

            L = GROUPS - 1
            wait(dve, scattered, L)
            dve.wait_ge(s_count, 1)
            plan = [0]

            def planned(ins):
                plan[0] += 1
                ins.then_inc(s_plan, 1)
                dve.wait_ge(s_plan, plan[0])

            planned(ve.tensor_copy(cnt, B5[:, 0:NE]))
            ve.memset(zeros, 0.0).then_inc(s_zero, 1)
            planned(ve.memset(one_e, 1.0))
            planned(ve.scalar_tensor_tensor(out=fill_f, in0=iota_e[:], scalar=float(REGION), in1=cnt, op0=ALU.mult, op1=ALU.add))
            ve.tensor_copy(fill_i, fill_f).then_inc(s_tab, 1)
            planned(ve.tensor_scalar(cnt_i, cnt, float(P - 1), None, ALU.add))
            planned(ve.tensor_scalar(nt_i, cnt_i, P.bit_length() - 1, None, ALU.arith_shift_right))
            planned(ve.tensor_copy(ntf, nt_i))
            planned(ve.tensor_tensor_scan(tend, one_e, ntf, 0.0, ALU.mult, ALU.add))
            planned(ve.tensor_tensor(tstart, tend, ntf, ALU.subtract))
            dve.wait_ge(s_const, 11)
            planned(ve.tensor_scalar(le, tend, pidx[:, 0:1], 0.0, ALU.is_le, ALU.add, accum_out=tab[:, 2:3]))
            planned(ve.tensor_scalar(tab[:, 3:4], tab[:, 2:3], float(NE), None, ALU.is_lt))
            planned(ve.scalar_tensor_tensor(out=le, in0=iota_e[:], scalar=tab[:, 2:3], in1=tstart, op0=ALU.is_equal,
                                            op1=ALU.mult, accum_out=tab[:, 4:5]))
            planned(ve.scalar_tensor_tensor(out=tab[:, 5:6], in0=pidx[:, 0:1], scalar=tab[:, 4:5], in1=tab[:, 3:4],
                                            op0=ALU.subtract, op1=ALU.mult))
            planned(ve.tensor_scalar(tab[:, 6:7], tab[:, 2:3], tab[:, 3:4], None, ALU.mult))
            ve.tensor_scalar(tab[:, 0:1], tab[:, 6:7], float(KH * P), None, ALU.mult).then_inc(s_plan, 1)
            ve.tensor_scalar(tab[:, 7:8], tab[:, 6:7], float(REGION), None, ALU.mult).then_inc(s_zero, 1)
            dve.wait_ge(s_zero, 2)
            ve.scalar_tensor_tensor(out=tab[:, 1:2], in0=tab[:, 5:6], scalar=float(P), in1=tab[:, 7:8],
                                    op0=ALU.mult, op1=ALU.add).then_inc(s_plan, 1)
            dve.wait_ge(s_tabp, 1)
            ve.tensor_copy(tab_i[0:1, :], B5[0:1, 0:2 * XT]).then_inc(s_tab, 1)

            sel = 0
            for n in range(TILES * TOP // 16):
                part16 = slice(n * 16, (n + 1) * 16)
                ve.tensor_tensor(selw, bc(iota_e[:], 1, 16), bc(idx_all[:, part16], 2, NE), ALU.is_equal).then_inc(s_sel, 1)
                dve.wait_ge(s_sel, sel + 1)
                ve.tensor_tensor(selw, selw, bc(tstart, 1, 16), ALU.mult).then_inc(s_sel, 1)
                dve.wait_ge(s_sel, sel + 2)
                ve.tensor_reduce(selp[:, part16], selw, AX.X, ALU.add).then_inc(s_sel, 1)
                dve.wait_ge(s_sel, sel + 3)
                sel += 3
            ve.scalar_tensor_tensor(out=pos2, in0=selp, scalar=float(P), in1=rank_all[:], op0=ALU.mult, op1=ALU.add)\
              .then_inc(s_sel, 1)

            def x_copy(i):
                wait(dve, xsp_done, i)
                wait(dve, gup_done, i - 1)
                ve.tensor_copy(xsT[:, 1, :], wide[:, QT * P:]).then_inc(xsT_ready.sem, 1)

            x_copy(0)
            with dve.Fori(0, ROUNDS) as i:
                wait(dve, sg_ready, i)
                wait(dve, aTp_done, i - 1)
                ve.tensor_tensor(act, sg, B2[:, :].rearrange("p (q f) -> p q f", q=QT)[:, :, FF:], ALU.mult)\
                  .then_inc(act_ready.sem, 1)
                x_copy(i + 1)
                wait(dve, aTp_done, i)
                wait(dve, down_done, i - 1)
                ve.tensor_copy(aT, B3[0:FF, :]).then_inc(aT_ready.sem, 1)
                wait(dve, down_done, i)
                wait(dve, ys_free, i - 1)
                ve.tensor_copy(ysb[:, 2:4, :], B5[:, :].rearrange("p (q d) -> p q d", q=2)).then_inc(ys_ready.sem, 1)

            with dve.Fori(0, GROUPS) as g:
                for j in range(KS):
                    wait(dve, shg_ready, g, j + 1)
                    wait(dve, shp_done, g, 2 * j + 2)
                    wait(dve, shd_done, g - 1)
                    ve.tensor_tensor(hid[:, j, :], shg[:, j, :], (B3, B5)[j % 2][:, 0:GT], ALU.mult).then_inc(hid_ready.sem, 1)
                for c in range(G2):
                    wait(dve, shd_done, g, c + 1)
                    wait(dve, fin_ready, g - 1)
                    ve.tensor_copy(comb[:, c, :], (B6, B7)[c][:, 0:H]).then_inc(comb_ready.sem, 1)
                    for k in range(TOP):
                        wait(dve, gathered[c * TOP + k], g)
                        wait(dve, comb_ready, g, c * (TOP + 1) + k + 1)
                        ve.scalar_tensor_tensor(out=comb[:, c, :], in0=yg[:, c * TOP + k, :],
                                                scalar=cw_all[:, bass.ds(g * (G2 * TOP) + (c * TOP + k), 1)],
                                                in1=comb[:, c, :], op0=ALU.mult, op1=ALU.add).then_inc(comb_ready.sem, 1)
                    wait(dve, comb_ready, g, (c + 1) * (TOP + 1))
                    wait(dve, fin_free, g - 1)
                    ve.tensor_tensor(fin[:, c, :], comb[:, c, :], gb_row[:], ALU.mult).then_inc(s_zero, 1)
                    dve.wait_ge(s_zero, g * G2 + (c + 3))
                    ve.tensor_tensor(fin[:, c, :], fin[:, c, :], x_all[:, g * G2 + c, :], ALU.add).then_inc(fin_ready.sem, 1)


def kernel(L0_attn_x, L0_attn_in_proj_w, L0_attn_conv_w, L0_attn_conv_b, L0_attn_dt_bias, L0_attn_A_log, L0_attn_D,
           L0_attn_norm_w, L0_attn_out_proj_w, L0_ffn_router_w, L0_ffn_router_bias, L0_ffn_wg, L0_ffn_wu, L0_ffn_wd,
           L0_ffn_swg, L0_ffn_swu, L0_ffn_swd, L0_c, L0_wmod):
    import numpy as np
    import concourse.bacc as bacc
    from concourse.bass_utils import run_bass_kernel_spmd as run_kernel

    arr = np.asarray

    def rows(v):
        return np.broadcast_to(arr(v)[None, :], (P, arr(v).shape[0]))

    def columns(v):
        return arr(v).reshape(-1, P).T

    conv = np.concatenate([arr(L0_attn_conv_w), arr(L0_attn_conv_b)[:, None]], axis=1)
    gu = np.concatenate([arr(L0_ffn_wg), arr(L0_ffn_wu)], axis=2)
    shared = [arr(w).transpose(1, 0, 2).reshape(H, SH) for w in (L0_ffn_swg, L0_ffn_swu)]
    data = {
        "x": arr(L0_attn_x).reshape(S, H),
        "w_in": arr(L0_attn_in_proj_w).T,
        "conv": conv.reshape(CJ, P, TAPS + 1).transpose(1, 0, 2),
        "rows8": np.stack([rows(v) for v in (L0_attn_dt_bias, L0_attn_A_log, L0_attn_D)], axis=1),
        "norm_w": columns(L0_attn_norm_w),
        "w_out": arr(L0_attn_out_proj_w).T,
        "w_router": arr(L0_ffn_router_w),
        "rbias": rows(L0_ffn_router_bias),
        "w_gu": gu.reshape(NE, KH, P, 2 * FF).transpose(2, 0, 1, 3).reshape(P, NE * KH * 2 * FF),
        "w_d": arr(L0_ffn_wd).transpose(1, 0, 2).reshape(FF, NE * H),
        "w_sgu": np.concatenate(shared, axis=1),
        "w_sd": arr(L0_ffn_swd).reshape(SH, H),
        "cvec": columns(arr(L0_c)[0]),
        "w_mod": arr(L0_wmod),
    }
    data = {n: np.ascontiguousarray(v) for n, v in data.items()}
    nc = bacc.Bacc("TRN2", target_bir_lowering=False, num_devices=1)
    args = [nc.dram_tensor(n, v.shape, F32, kind="ExternalInput").ap() for n, v in data.items()]
    args.append(nc.dram_tensor("out", (S, H), F32, kind="ExternalOutput").ap())
    build(nc, *args)
    return run_kernel(nc, [data], core_ids=[0]).results[0]["out"].reshape(1, S, H)
```

```python
from contextlib import ExitStack

import concourse.bass as bass
from concourse import mybir

F32 = mybir.dt.float32
I32 = mybir.dt.int32
U32 = mybir.dt.uint32
ALU = mybir.AluOpType
ACT = mybir.ActivationFunctionType
AX = mybir.AxisListType

P = 128
S = 2048
H = 256
KH = H // P
EI = 512
KE = EI // P
NH, HP, N = 8, 64, 64
CONV = EI + 2 * N
CJ = CONV // P
TAPS = 4
PROJ = EI + CONV + NH
G2 = 2
GT = G2 * P
GROUPS = S // GT
TILES = S // P
NE, FF, TOP = 64, 64, 4
REGION = S + P
XT = 128
QT = 4
ROUNDS = XT // QT
EARLY = 2
SH = 512
KS = SH // P
LN_EPS = 1e-5
RMS_EPS = 1e-6
ARENA = 25900


class Event:
    def __init__(self, sem, per, ahead=1):
        self.sem, self.per, self.ahead = sem, per, ahead

    def at(self, g, k=None):
        return (g + self.ahead) * self.per + (self.per if k is None else k)


def bc(ap, axis, n):
    wide = ap.unsqueeze(axis)
    shape = list(wide.shape)
    shape[axis] = n
    return wide.broadcast_to(shape)


def build(nc, x, w_in, conv, rows8, norm_w, w_out, w_router, rbias, w_gu, w_d, w_sgu, w_sd, cvec, w_mod, d_cols, out):
    with ExitStack() as ctx:
        def sb(name, shape, dt=F32):
            return ctx.enter_context(nc.sbuf_tensor(name, shape, dt))

        def sem(name):
            return ctx.enter_context(nc.semaphore(name))

        events = []

        def event(name, per, ahead=1):
            events.append(Event(sem(name), per, ahead))
            return events[-1]

        def dma_event(name, dmas=1):
            return Event(sem(name), 16 * dmas, ahead=0)

        expert_in = nc.dram_tensor("expert_in", (NE * REGION, H), F32).ap()
        expert_out = nc.dram_tensor("expert_out", (XT * P, H), F32).ap()

        bank = [ctx.enter_context(nc.psum_tensor(f"bank{b}", [P, 512], F32)) for b in (2, 3, 4, 5, 6, 7)]
        wide = ctx.enter_context(nc.psum_tensor("wide", [P, 1024], F32))
        B2, B3, B4, B5, B6, B7 = bank
        up_bank = (B2, B3, B4, B6)

        x_all = sb("x_all", [P, TILES, H])
        h2T_all = sb("h2T_all", [P, KH, S])
        gu = sb("gu", [P, NE * KH * P])
        ident = sb("ident", [P, P])
        ones = sb("ones", [P, P])
        gb_row = sb("gb_row", [P, H])
        idx_all = sb("idx_all", [P, TILES * TOP])
        rank_all = sb("rank_all", [P, TILES * TOP])
        cw_all = sb("cw_all", [P, TILES * TOP])
        run = sb("run", [P, NE])
        iota_e = sb("iota_e", [P, NE])
        neg_half = sb("neg_half", [P, 2])
        pidx = sb("pidx", [P, 1])
        zeros = sb("zeros", [P, H])
        diag_d = sb("diag_d", [P, KE, P])
        cnt = sb("cnt", [P, NE])
        cnt_i = sb("cnt_i", [P, NE], I32)
        nt_i = sb("nt_i", [P, NE], I32)
        ntf = sb("ntf", [P, NE])
        one_e = sb("one_e", [P, NE])
        tend = sb("tend", [P, NE])
        tstart = sb("tstart", [P, NE])
        last = sb("last", [P, NE])
        pack = sb("pack", [P, NE])
        le = sb("le", [P, NE])
        tab = sb("tab", [P, 12])
        tab_i = sb("tab_i", [1, 2 * XT], I32)
        pk_all = sb("pk_all", [P, TILES * TOP])

        arena = sb("arena", [P, ARENA])
        top = [0]

        def part(*shape, dt=F32, rows=P, of=arena, size=ARENA):
            n = 1
            for d in shape:
                n *= d
            assert top[0] + n <= size, (top[0], n)
            a = of[0:rows, top[0]:top[0] + n]
            top[0] += n + n % 2
            if dt != F32:
                a = a.bitcast(dt)
            if len(shape) == 2:
                a = a.rearrange("p (a b) -> p a b", b=shape[1])
            if len(shape) == 3:
                a = a.rearrange("p (a b c) -> p a b c", b=shape[1], c=shape[2])
            return a

        wi = part(KH, PROJ)
        z1 = part(G2, H)
        hT = part(KH, GT)
        cin = part(CJ, GT + TAPS - 1)
        acc = part(CJ, GT)
        wo = part(KE, H)
        wr = part(KH, NE)
        rb = part(NE)
        cvw = part(CJ, TAPS + 1)
        r8 = part(2, NH)
        dcol = part(KE)
        nw = part(KE)
        tri = part(P)
        strict = part(P)
        before = part(P)
        iota8 = part(8, NE)
        cb_row = part(H)
        sb_row = part(H)
        ga_row = part(H)
        col1 = part(2 * KH)
        c_in = part(KH)
        c_silu = part(KH)
        neg_a = part(NH)
        st6 = part(G2, 6)
        mv1 = part(G2, 2)
        ve1 = part(2)
        rstd1 = part(2)
        xc = part(KE, GT)
        BT = part(GT, rows=N)
        CT = part(GT, rows=N)
        gs = part(G2, EI)
        dts = part(G2, NH)
        dtx = part(G2, NH)
        nab = part(G2, NH)
        lnp = part(G2, NH)
        dt = part(G2, NH)
        av = part(G2, NH)
        am = part(NH, P)
        ed = part(G2, 3 * NH)
        gb = part(G2, P + N)
        gm = part(G2, P)
        E = [part(NH, P) for _ in range(G2)]
        mod_at = top[0]
        xTs = part(G2, EI)
        xdt = part(G2, EI)
        xdd = part(G2, EI)
        y = part(G2, EI)
        yT = part(G2, EI)
        state = part(EI, rows=N)
        junk = part(EI)
        ssq = part(2)
        vy = part(2)
        rstdy = part(2)
        x1 = part(G2, H)
        st6b = part(G2, 6)
        mv2 = part(G2, 2)
        ve2 = part(2)
        rstd2 = part(2)
        h2 = part(G2, H)
        h2T = part(KH, GT)
        h2s = part(G2, H)
        lgs = part(G2, NE)
        lb = part(G2, NE)
        nm = part(2)
        el = part(G2, NE)
        m8 = part(G2, 8)
        ix8 = part(G2, 8, dt=U32)
        ixf = part(G2 * TOP)
        oh = part(G2 * TOP, NE)
        ohe = part(G2 * TOP, NE)
        ohr = part(G2 * TOP, NE)
        mask = part(G2, NE)
        cw = part(G2 * TOP)
        csum = part(2)
        rcs = part(2)
        rank = part(G2 * TOP)
        pos = part(G2 * TOP, dt=U32)
        wm = arena[:, mod_at:mod_at + KH * 6 * H].rearrange("p (k n) -> p k n", k=KH)

        top[0] = 0
        wsh = part(KH, 2 * SH)
        wsd = part(KS, H)
        second_at = top[0]
        sg = part(QT, FF)
        act = part(QT, FF)
        ysb = [part(QT, H) for _ in range(2)]
        top[0] = second_at
        sh_x = part(G2, H)
        shg = part(KS, GT)
        hid = part(KS, GT)
        assert top[0] <= KH * PROJ + G2 * H + KH * GT + CJ * (2 * GT + TAPS - 1)
        wd = part(NE * H, rows=FF)
        selw = [part(2, NE) for _ in range(2)]
        xsT = part(KH, QT * P)
        aT = part(QT * P, rows=FF)
        rows_at = top[0]
        xsb = [part(QT, H) for _ in range(2)]
        top[0] = rows_at
        pk_i = part(TILES * TOP, dt=I32)
        st_i = part(TILES * TOP, dt=I32)
        n_i = part(TILES * TOP, dt=I32)
        st_f = part(TILES * TOP)
        n_f = part(TILES * TOP)
        back = part(TILES * TOP)
        inlast = part(TILES * TOP)
        pos2 = part(TILES * TOP, dt=U32)
        top[0] = 0
        third = {"of": gu, "size": NE * KH * P}
        yg = [part(G2 * TOP, H, **third) for _ in range(2)]
        comb = part(G2, H, **third)
        fin = part(G2, H, **third)

        s_x = sem("x_loaded")
        s_w = sem("weights_loaded")
        s_const = sem("constants_made")
        s_vec = sem("vector_setup")
        s_csilu = sem("c_silu_ready")
        s_modp = sem("mod_in_psum")
        s_mod = sem("mod_ready")
        s_gu = sem("gate_up_loaded")
        s_alone = sem("wait_alone")
        NW = 12

        stats1 = event("stats1", 2)
        mv1_ready = event("mv1_ready", 2)
        ve1_ready = event("ve1_ready", 1)
        rstd1_ready = event("rstd1_ready", 1)
        z1_ready = event("z1_ready", 2)
        z1T_done = event("z1T_done", 1)
        hT_ready = event("hT_ready", 2)
        convp_done = event("convp_done", 3)
        cin_ready = event("cin_ready", 3)
        dts_ready = event("dts_ready", 1)
        halo_saved = event("halo_saved", 1)
        tap_done = event("tap_done", CJ * (TAPS - 1))
        gatep_done = event("gatep_done", 2)
        xc_ready = event("xc_ready", 3)
        gs_ready = event("gs_ready", 2)
        dtx_ready = event("dtx_ready", 2)
        dte_ready = event("dte_ready", 2)
        dt_ready = event("dt_ready", 2)
        am_ready = event("am_ready", 2)
        sm_done = event("small_products_done", 2)
        gb_ready = event("gb_ready", 4)
        gm_ready = event("gm_ready", 2)
        seg_done = event("seg_done", 2)
        E_ready = event("E_ready", 2)
        M_ready = event("M_ready", 2)
        xT_done = event("xT_done", 2)
        xTs_ready = event("xTs_ready", 2)
        xdt_ready = event("xdt_ready", 2)
        xdd_ready = event("xdd_ready", 2)
        tap0_done = event("tap0_done", CJ)
        yd_done = event("yd_done", 2)
        yo_done = event("yo_done", 2)
        sn_done = event("sn_done", 2)
        smul_done = event("state_scaled", 2)
        state_ready = event("state_ready", 2)
        y1_done = event("y1_done", 2)
        y2_done = event("y2_done", 2)
        yf_done = event("yf_done", 2)
        ssq_ready = event("ssq_ready", 2)
        vy_ready = event("vy_ready", 1)
        rstdy_ready = event("rstdy_ready", 1)
        yT_done = event("yT_done", 2)
        yTs_ready = event("yTs_ready", 2)
        op_done = event("op_done", 2)
        att_done = event("att_done", 2)
        x1_ready = event("x1_ready", 2)
        stats2 = event("stats2", 2)
        mv2_ready = event("mv2_ready", 2)
        ve2_ready = event("ve2_ready", 1)
        rstd2_ready = event("rstd2_ready", 1)
        h2_step = event("h2_step", 4)
        h2_ready = event("h2_ready", 2)
        h2T_done = event("h2T_done", 1)
        h2T_ready = event("h2T_ready", 1)
        h2T_kept = event("h2T_kept", 1)
        lg_done = event("lg_done", 1)
        lgs_ready = event("lgs_ready", 1)
        lb_ready = event("lb_ready", 1)
        nm_ready = event("nm_ready", 1)
        el_ready = event("el_ready", 2)
        m8_ready = event("m8_ready", 2)
        ix_ready = event("ix_ready", 2)
        ixf_ready = event("ixf_ready", 1)
        oh_ready = event("oh_ready", 1)
        mask_ready = event("mask_ready", 1)
        rank_done = event("rank_done", 1)
        ohr_ready = event("ohr_ready", 1)
        rank_ready = event("rank_ready", 1)
        pos_ready = event("pos_ready", 1)
        h2s_ready = event("h2_rows_copied", 1)
        run_ready = event("run_ready", 2)
        scattered = dma_event("scattered", G2 * TOP)
        rows_free = event("scattered_rows_free", 1)
        cw_steps = event("cw_steps", 5)

        s_count = sem("counts_in_psum")
        s_plan = sem("plan_steps")
        s_tabp = sem("table_in_psum")
        s_tab = sem("table_ready")
        s_fill = sem("padding_filled")
        s_wd = sem("down_loaded")
        s_wsh = sem("shared_loaded")
        s_zero = sem("zeros_ready")
        s_cols = sem("table_columns")
        xs_loaded = [[dma_event(f"xs{q}{p}_loaded") for p in range(2)] for q in range(QT)]
        xsp_done = event("xs_transposed", 1, ahead=2)
        xsT_ready = event("xsT_ready", 2)
        gup_done = event("gate_up_done", 1)
        sg_ready = event("sg_ready", 1)
        act_ready = event("act_ready", 1)
        aTp_done = event("act_transposed", 1)
        aT_ready = event("aT_ready", 1)
        down_done = event("down_done", 2)
        ys_ready = event("ys_ready", 2)
        ys_stored = [dma_event(f"ys{p}_stored") for p in range(2)]
        sel_steps = event("sel_steps", 3)
        s_sel = sem("gather_rows_steps")
        shp_done = event("shared_up_done", KS)
        shg_ready = event("shared_gate_ready", KS)
        hid_ready = event("hid_ready", KS)
        shd_done = event("shared_down_done", 2)
        shx_ready = event("shared_scaled", 2)
        base_ready = event("shared_added", 2)
        comb_ready = event("comb_ready", 2 * TOP)
        fin_steps = event("fin_steps", 2)
        fin_ready = event("fin_ready", 2)
        gathered = [[dma_event(f"gathered{k}{p}") for p in range(2)] for k in range(G2 * TOP)]
        stored = dma_event("stored")
        fin_free = event("fin_free", 1)

        block = ctx.enter_context(nc.Block())

        def wait(eng, ev, g, k=None):
            count = ev.at(g, k)
            if not isinstance(count, int) or count > 0:
                eng.wait_ge(ev.sem, count)

        def wait_alone(eng, ev, g, k=None):
            eng.wait_ge(ev.sem, ev.at(g, k))
            eng.sem_inc(s_alone, 1)

        def staggered(eng, step):
            def at(i):
                step(*(g if 0 <= g < GROUPS else None for g in (i - 3, i - 2, i - 1, i, i + 1)))

            for i in range(-1, 3):
                at(i)
            with eng.Fori(3, GROUPS - 1) as i:
                step(i - 3, i - 2, i - 1, i, i + 1)
            for i in range(GROUPS - 1, GROUPS + 3):
                at(i)

        def tok(c):
            return slice(c * P, (c + 1) * P)

        @block.sync
        def _(sp):
            for ev in events:
                sp.sem_inc(ev.sem, ev.per * ev.ahead)
            sp.dma_start(x_all[:], x.rearrange("(t p) d -> p t d", p=P)).then_inc(s_x, 16)
            sp.dma_start(c_in, cvec).then_inc(s_w, 16)
            sp.dma_start(wm, w_mod.rearrange("(k p) n -> p k n", p=P)).then_inc(s_w, 16)
            sp.dma_start(wi, w_in.rearrange("(k p) n -> p k n", p=P)).then_inc(s_w, 16)
            sp.dma_start(cvw, conv).then_inc(s_w, 16)
            sp.dma_start(r8, rows8).then_inc(s_w, 16)
            sp.dma_start(nw, norm_w).then_inc(s_w, 16)
            sp.dma_start(wo, w_out.rearrange("(k p) n -> p k n", p=P)).then_inc(s_w, 16)
            sp.dma_start(wr, w_router.rearrange("(k p) n -> p k n", p=P)).then_inc(s_w, 16)
            sp.dma_start(rb, rbias).then_inc(s_w, 16)
            sp.dma_start(dcol, d_cols).then_inc(s_w, 16)
            sp.wait_ge(s_zero, 1)
            sp.dma_start(expert_in.rearrange("(e r) d -> r e d", e=NE)[0:P, :, :], bc(zeros[:], 1, NE)).then_inc(s_fill, 16)
            sp.dma_start(gu[:], w_gu).then_inc(s_gu, 16)
            with sp.Fori(0, GROUPS - 1) as g:
                wait(sp, scattered, g)
                sp.sem_inc(rows_free.sem, 1)

            L = GROUPS - 1
            wait(sp, gatep_done, L)
            wait(sp, halo_saved, L)
            wait(sp, xc_ready, L)
            sp.dma_start(wsh, w_sgu.rearrange("(k p) n -> p k n", p=P)).then_inc(s_wsh, 16)
            sp.dma_start(wsd, w_sd.rearrange("(k p) n -> p k n", p=P)).then_inc(s_wsh, 16)
            wait(sp, cw_steps, L)
            wait(sp, pos_ready, L)
            wait(sp, h2s_ready, L)
            wait(sp, run_ready, L)
            wait(sp, scattered, L)
            sp.dma_start(wd, w_d).then_inc(s_wd, 16)
            sp.wait_ge(s_tab, 1)

            def load(i, p):
                r = i * 2 + p
                rows = [sp.value_load(tab_i[0:1, bass.ds(r * QT + (XT + q), 1)], min_val=0, max_val=NE * REGION - P)
                        for q in range(2)]
                wait(sp, xsp_done, r - 2)
                for q in range(2):
                    sp.dma_start(xsb[p][:, q, :], expert_in[bass.ds(rows[q], P), :]).then_inc(xs_loaded[q][p].sem, 16)

            with sp.Fori(0, ROUNDS // 2) as i:
                for p in range(2):
                    load(i, p)
            with sp.Fori(0, GROUPS) as g:
                wait(sp, fin_ready, g)
                sp.dma_start(out[bass.ds(g * GT, GT), :].rearrange("(c p) d -> p c d", p=P), fin).then_inc(stored.sem, 16)
                wait(sp, stored, g)
                sp.sem_inc(fin_free.sem, 1)

        @block.gpsimd
        def _(pool):
            pool_ = nc.gpsimd
            pool_.memset(zeros[:], 0.0).then_inc(s_zero, 1)
            pool_.memset(ident[:], 0.0).then_inc(s_const, 1)
            pool_.memset(ones[:], 1.0).then_inc(s_const, 1)
            pool_.memset(run[:], 0.0).then_inc(s_const, 1)
            pool_.memset(neg_half[:], -0.5).then_inc(s_const, 1)
            pool_.iota(iota_e[:], [[1, NE]], base=0, channel_multiplier=0,
                       allow_small_or_imprecise_dtypes=True).then_inc(s_const, 1)
            pool_.iota(iota8, [[0, 8], [1, NE]], base=0, channel_multiplier=0,
                       allow_small_or_imprecise_dtypes=True).then_inc(s_const, 1)
            pool.wait_ge(s_const, 6)
            pool_.affine_select(out=ident[:], in_=ident[:], compare_op=ALU.not_equal, fill=1.0, base=0,
                                pattern=[[-1, P]], channel_multiplier=1).then_inc(s_const, 1)
            pool_.affine_select(out=tri, in_=ones[:], compare_op=ALU.is_ge, fill=0.0, base=0,
                                pattern=[[1, P]], channel_multiplier=-1).then_inc(s_const, 1)
            pool_.affine_select(out=strict, in_=ones[:], compare_op=ALU.is_gt, fill=0.0, base=0,
                                pattern=[[-1, P]], channel_multiplier=1).then_inc(s_const, 1)
            pool_.affine_select(out=before, in_=ones[:], compare_op=ALU.is_gt, fill=0.0, base=0,
                                pattern=[[1, P]], channel_multiplier=-1).then_inc(s_const, 1)
            pool_.iota(pidx[:], [[0, 1]], base=0, channel_multiplier=1,
                       allow_small_or_imprecise_dtypes=True).then_inc(s_const, 1)
            pool.wait_ge(s_const, 11)
            pool.wait_ge(s_w, 16 * (NW - 2))
            pool.wait_ge(s_modp, 8)
            pool.wait_ge(s_mod, 3)
            pool.wait_ge(s_fill, 16)

            def rsqrt_front(f):
                wait(pool, ve1_ready, f)
                wait(pool, z1_ready, f - 1)
                pool_.tensor_tensor(rstd1, ve1, neg_half[:], ALU.pow).then_inc(rstd1_ready.sem, 1)

            def mix_inputs(g, c):
                wait(pool, dt_ready, g)
                if c:
                    wait(pool, seg_done, g, c)
                else:
                    wait(pool, seg_done, g - 1)
                pool_.tensor_tensor(am, bc(av[:, c, :], 2, P), bc(strict, 1, NH), ALU.mult).then_inc(am_ready.sem, 1)

            def mix_values(g, c):
                xs = xTs[:, c, :].rearrange("p (h d) -> p h d", d=HP)
                o = xdt[:, c, :].rearrange("p (h d) -> p h d", d=HP)
                wait(pool, xTs_ready, g, c + 1)
                wait(pool, yd_done, g - 1, c + 1)
                pool_.tensor_tensor(o, xs, bc(dt[:, c, :], 2, HP), ALU.mult).then_inc(xdt_ready.sem, 1)
                wait(pool, xdt_ready, g, c + 1)
                wait(pool, gb_ready, g, 2 * c + 1)
                wait(pool, sn_done, g - 1, c + 1)
                pool_.tensor_tensor(xdd[:, c, :].rearrange("p (h d) -> p h d", d=HP), o, bc(ed[:, c, NH:2 * NH], 2, HP),
                                    ALU.mult).then_inc(xdd_ready.sem, 1)

            def gate(g, c):
                wait(pool, y2_done, g, c + 1)
                wait(pool, gs_ready, g, c + 1)
                pool_.tensor_tensor(y[:, c, :], y[:, c, :], gs[:, c, :], ALU.mult).then_inc(yf_done.sem, 1)

            def rsqrt_rms(g):
                wait(pool, vy_ready, g)
                wait(pool, att_done, g - 1)
                pool_.tensor_tensor(rstdy, vy, neg_half[:], ALU.pow).then_inc(rstdy_ready.sem, 1)

            def rsqrt_route(g):
                wait(pool, ve2_ready, g)
                wait(pool, h2_step, g - 1)
                pool_.tensor_tensor(rstd2, ve2, neg_half[:], ALU.pow).then_inc(rstd2_ready.sem, 1)

            def count(g):
                wait(pool, rank_done, g)
                wait(pool, run_ready, g - 1)
                pool_.tensor_tensor(run[:], run[:], mask[:, 0, :], ALU.add).then_inc(run_ready.sem, 1)
                wait(pool, run_ready, g, 1)
                pool_.tensor_tensor(run[:], run[:], mask[:, 1, :], ALU.add).then_inc(run_ready.sem, 1)

            def scatter(g):
                wait_alone(pool, pos_ready, g)
                wait_alone(pool, h2s_ready, g)
                for c in range(G2):
                    for k in range(TOP):
                        j = c * TOP + k
                        pool_.indirect_dma_start(expert_in, bass.IndirectOffsetOnAxis(ap=pos[:, j:j + 1], axis=0),
                                                 h2s[:, c, :], None).then_inc(scattered.sem, 16)

            def step(s, q, r, g, f):
                if g is not None:
                    mix_inputs(g, 0)
                if f is not None:
                    rsqrt_front(f)
                if r is not None:
                    rsqrt_rms(r)
                if g is not None:
                    mix_values(g, 0)
                    mix_inputs(g, 1)
                    mix_values(g, 1)
                if r is not None:
                    rsqrt_route(r)
                if s is not None:
                    scatter(s)
                if g is not None:
                    gate(g, 0)
                    gate(g, 1)
                if q is not None:
                    count(q)

            staggered(pool, step)

            pool.wait_ge(s_tab, 1)
            wait(pool, scattered, GROUPS - 1)

            def load(i, p):
                r = i * 2 + p
                rows = [pool.value_load(tab_i[0:1, bass.ds(r * QT + (XT + q), 1)], min_val=0, max_val=NE * REGION - P)
                        for q in (2, 3)]
                wait_alone(pool, xsp_done, r - 2)
                for q in (2, 3):
                    pool.dma_start(xsb[p][:, q, :], expert_in[bass.ds(rows[q - 2], P), :]).then_inc(xs_loaded[q][p].sem, 16)

            with pool.Fori(0, ROUNDS // 2) as i:
                for p in range(2):
                    load(i, p)

            pool.wait_ge(s_sel, 11)
            for p in range(2):
                wait(pool, ys_stored[p], ROUNDS // 2 - 1)
            for g in range(GROUPS):
                for c in range(G2):
                    for k in range(TOP):
                        j = c * TOP + k
                        at = (g * G2 + c) * TOP + k
                        if g >= 2:
                            wait(pool, comb_ready, g - 2, j + 1)
                        pool_.indirect_dma_start(yg[g % 2][:, j, :], None, expert_out[:, :],
                                                 bass.IndirectOffsetOnAxis(ap=pos2[:, at:at + 1], axis=0))\
                             .then_inc(gathered[j][g % 2].sem, 16)

        @block.scalar
        def _(act_e):
            a = act_e
            sc = nc.scalar
            a.wait_ge(s_w, 16 * (NW - 2))
            sc.activation(c_silu, c_in, ACT.Silu).then_inc(s_csilu, 1)
            sc.activation(neg_a, r8[:, 1, :], ACT.Exp).then_inc(s_csilu, 1)
            a.wait_ge(s_vec, 2)

            def front_hT(f):
                wait(a, z1T_done, f)
                wait(a, gatep_done, f - 1)
                for k in range(KH):
                    sc.activation(hT[:, k, :], B6[:, k * GT:(k + 1) * GT], ACT.Identity, bias=col1[:, k:k + 1],
                                  scale=col1[:, KH + k:KH + k + 1]).then_inc(hT_ready.sem, 1)

            def taps0(f, js):
                for j in js:
                    wait(a, cin_ready, f, j // 2 + 1)
                    wait(a, xc_ready, f - 1)
                    sc.activation(acc[:, j, :], cin[:, j, 0:GT], ACT.Identity, bias=cvw[:, j, TAPS:TAPS + 1],
                                  scale=cvw[:, j, 0:1]).then_inc(tap0_done.sem, 1)

            def front_conv_in(f):
                wait(a, halo_saved, f - 1)
                for n, b in enumerate((B7, B6)):
                    wait(a, convp_done, f, n + 1)
                    sc.activation(cin[:, 2 * n:2 * n + 2, TAPS - 1:], b[:, :].rearrange("p (j t) -> p j t", j=2),
                                  ACT.Copy).then_inc(cin_ready.sem, 1)
                    taps0(f, (2 * n, 2 * n + 1))
                wait(a, convp_done, f, 3)
                wait(a, dtx_ready, f - 1)
                sc.activation(cin[:, 4, TAPS - 1:], B7[:, 0:GT], ACT.Copy).then_inc(cin_ready.sem, 1)
                sc.activation(dts, B7[:, GT:GT + G2 * NH].rearrange("p (c h) -> p c h", c=G2), ACT.Copy)\
                  .then_inc(dts_ready.sem, 1)
                taps0(f, (4,))

            def front_silu(f):
                wait(a, yo_done, f - 1)
                wait(a, xT_done, f - 1)
                wait(a, yd_done, f - 1)
                wait(a, tap_done, f)
                sc.activation(xc, acc[:, 0:KE, :], ACT.Silu).then_inc(xc_ready.sem, 1)
                sc.activation(BT, acc[0:N, KE, :], ACT.Silu).then_inc(xc_ready.sem, 1)
                sc.activation(CT, acc[N:P, KE, :], ACT.Silu).then_inc(xc_ready.sem, 1)
                for c, b in enumerate((B6, B7)):
                    wait(a, gatep_done, f, c + 1)
                    wait(a, yf_done, f - 1, c + 1)
                    sc.activation(gs[:, c, :], b[:, :], ACT.Silu).then_inc(gs_ready.sem, 1)

            def front_exp(f):
                wait(a, dtx_ready, f)
                sc.activation(lnp, nab, ACT.Exp).then_inc(dte_ready.sem, 1)

            def front_ln(f):
                wait(a, dte_ready, f, 1)
                sc.activation(lnp, lnp, ACT.Ln, bias=1.0).then_inc(dte_ready.sem, 1)

            def mix_small(g, c):
                wait(a, sm_done, g, c + 1)
                wait(a, y1_done, g - 1, c + 1)
                wait(a, smul_done, g - 1, c + 1)
                wait(a, xdd_ready, g - 1, c + 1)
                sc.activation(ed[:, c, :], B2[:, 0:3 * NH], ACT.Exp).then_inc(gb_ready.sem, 1)
                wait(a, gm_ready, g - 1, c + 1)
                wait(a, sn_done, g - 1, c + 1)
                sc.activation(gb[:, c, :], B2[:, P:2 * P + N], ACT.Copy).then_inc(gb_ready.sem, 1)

            def mix_xT(g, c):
                wait(a, xT_done, g, c + 1)
                wait(a, xdt_ready, g - 1, c + 1)
                sc.activation(xTs[:, c, :], B3[:, :], ACT.Copy).then_inc(xTs_ready.sem, 1)

            def mix_E(g, c):
                wait(a, seg_done, g, c + 1)
                wait(a, yd_done, g - 1, c + 1)
                sc.activation(E[c], wide[:, :].rearrange("p (h l) -> p h l", l=P), ACT.Exp).then_inc(E_ready.sem, 1)

            def mix_square(g, c):
                wait(a, yf_done, g, c + 1)
                wait(a, vy_ready, g - 1)
                if c:
                    wait(a, ssq_ready, g, c)
                else:
                    wait(a, ssq_ready, g - 1)
                sc.activation(junk, y[:, c, :], ACT.Square, accum_out=ssq[:, c:c + 1]).then_inc(ssq_ready.sem, 1)

            def mix_yT(g, c):
                wait(a, yT_done, g, c + 1)
                wait(a, op_done, g - 1, c + 1)
                sc.activation(yT[:, c, :], B3[:, :], ACT.Copy).then_inc(yTs_ready.sem, 1)

            def route_h2T(g):
                wait(a, lg_done, g - 1)
                wait(a, h2T_kept, g - 1)
                wait(a, h2T_done, g)
                sc.activation(h2T, B3[:, :].rearrange("p (k t) -> p k t", k=KH), ACT.Copy).then_inc(h2T_ready.sem, 1)

            def keep_h2T(g):
                wait(a, h2T_ready, g)
                sc.activation(h2T_all[:, :, bass.ds(g * GT, GT)], h2T, ACT.Copy).then_inc(h2T_kept.sem, 1)

            def route_exp(g):
                wait(a, nm_ready, g)
                wait(a, cw_steps, g - 1)
                for c in range(G2):
                    sc.activation(el[:, c, :], lgs[:, c, :], ACT.Exp, bias=nm[:, c:c + 1]).then_inc(el_ready.sem, 1)

            def step(s, q, r, g, f):
                if g is not None:
                    mix_small(g, 0)
                    mix_xT(g, 0)
                    mix_E(g, 0)
                if r is not None:
                    mix_yT(r, 0)
                if g is not None:
                    mix_small(g, 1)
                if q is not None:
                    route_h2T(q)
                if g is not None:
                    mix_xT(g, 1)
                    mix_E(g, 1)
                if f is not None:
                    front_hT(f)
                if r is not None:
                    mix_yT(r, 1)
                if q is not None:
                    route_exp(q)
                    keep_h2T(q)
                if f is not None:
                    front_conv_in(f)
                    front_exp(f)
                if g is not None:
                    mix_square(g, 0)
                if f is not None:
                    front_ln(f)
                    front_silu(f)
                if g is not None:
                    mix_square(g, 1)

            staggered(a, step)

            def shared(g):
                for j in range(KS):
                    wait(a, shp_done, g, j + 1)
                    wait(a, hid_ready, g - 1, j + 1)
                    sc.activation(shg[:, j, :], up_bank[j][:, 0:GT], ACT.Silu).then_inc(shg_ready.sem, 1)

            wait(a, halo_saved, GROUPS - 1)
            wait(a, gatep_done, GROUPS - 1)
            for g in range(EARLY):
                shared(g)
            wait(a, scattered, GROUPS - 1)

            def x_copy(r):
                wait(a, xsp_done, r)
                wait(a, gup_done, r - 1)
                sc.activation(xsT[:, 0, :], wide[:, 0:QT * P], ACT.Copy).then_inc(xsT_ready.sem, 1)

            def store(i, p):
                r = i * 2 + p
                wait(a, ys_ready, r)
                a.dma_start(expert_out[bass.ds(r * (QT * P), QT * P), :].rearrange("(q p) d -> p q d", p=P), ysb[p])\
                 .then_inc(ys_stored[p].sem, 16)

            def round_(i, p, more=True):
                r = i * 2 + p
                wait(a, gup_done, r)
                wait(a, act_ready, r - 1)
                sc.activation(sg, B2[:, :].rearrange("p (q f) -> p q f", q=QT)[:, :, 0:FF], ACT.Silu).then_inc(sg_ready.sem, 1)
                if more:
                    x_copy(r + 1)

            def rows_out(i, p):
                r = i * 2 + p
                wait(a, down_done, r, 1)
                wait(a, ys_stored[p], i - 1)
                sc.activation(ysb[p][:, 0:2, :], B4[:, :].rearrange("p (q d) -> p q d", q=2), ACT.Copy).then_inc(ys_ready.sem, 1)
                store(i, p)

            last_i = ROUNDS // 2 - 1
            def two_rounds(i):
                round_(i, 1)
                rows_out(i, 0)
                round_(i + 1, 0)
                rows_out(i, 1)

            x_copy(0)
            round_(0, 0)
            two_rounds(0)
            with a.Fori(1, last_i) as i:
                two_rounds(i)
            round_(last_i, 1, more=False)
            rows_out(last_i, 0)
            rows_out(last_i, 1)

            for p in range(2):
                wait(a, ys_stored[p], last_i)
            with a.Fori(EARLY, GROUPS) as g:
                shared(g)

        @block.tensor
        def _(pe):
            te = nc.tensor

            pe.wait_ge(s_csilu, 1)
            pe.wait_ge(s_const, 10)
            for n in range(2 * KH):
                for k in range(KH):
                    mm = te.matmul(B2[:, n:n + 1], wm[:, k, n * P:(n + 1) * P], c_silu[:, k:k + 1],
                                   start=(k == 0), stop=(k == KH - 1))
            mm.then_inc(s_modp, 4)
            for n, b in ((2, B4), (3, B5), (4, B6), (5, B7)):
                for k in range(KH):
                    mm = te.matmul(b[:, 0:H], c_silu[:, k:k + 1].broadcast_to([P, P]), wm[:, k, n * H:(n + 1) * H],
                                   start=(k == 0), stop=(k == KH - 1))
                mm.then_inc(s_modp, 1)
            pe.wait_ge(s_mod, 15)

            def front_zT(f):
                wait(pe, z1_ready, f)
                wait(pe, gs_ready, f - 1)
                for k in range(KH):
                    for c in range(G2):
                        mm = te.transpose(B6[:, k * GT + c * P:k * GT + (c + 1) * P], z1[:, c, k * P:(k + 1) * P], ident[:])
                mm.then_inc(z1T_done.sem, 1)

            def front_conv(f):
                wait(pe, hT_ready, f)
                for n, b in enumerate((B7, B6, B7)):
                    if n == 2:
                        wait(pe, cin_ready, f, 1)
                    for j in range(2 * n, min(2 * n + 2, CJ)):
                        for k in range(KH):
                            mm = te.matmul(b[:, (j % 2) * GT:(j % 2 + 1) * GT], wi[:, k, EI + j * P:EI + (j + 1) * P],
                                           hT[:, k, :], start=(k == 0), stop=(k == KH - 1))
                    if n < 2:
                        mm.then_inc(convp_done.sem, 1)
                for c in range(G2):
                    for k in range(KH):
                        mm = te.matmul(B7[:, GT + c * NH:GT + (c + 1) * NH], hT[:, k, tok(c)], wi[:, k, PROJ - NH:PROJ],
                                       start=(k == 0), stop=(k == KH - 1))
                mm.then_inc(convp_done.sem, 1)

            def front_gate(f, c):
                wait(pe, cin_ready, f, 2 + c)
                if c:
                    wait(pe, dts_ready, f)
                for k in range(KH):
                    mm = te.matmul((B6, B7)[c][:, :], hT[:, k, tok(c)], wi[:, k, 0:EI], start=(k == 0), stop=(k == KH - 1))
                mm.then_inc(gatep_done.sem, 1)

            def mix_small(g, c):
                wait(pe, dt_ready, g)
                wait(pe, xc_ready, g)
                if c:
                    wait(pe, gb_ready, g, 2 * c)
                else:
                    wait(pe, gb_ready, g - 1)
                for n, m in enumerate((tri, strict, ones[:])):
                    te.matmul(B2[:, n * NH:(n + 1) * NH], m, av[:, c, :], start=True, stop=True)
                te.matmul(B2[:, P:2 * P], BT[:, tok(c)], CT[:, tok(c)], start=True, stop=True)
                te.transpose(B2[:, 2 * P:2 * P + N], BT[:, tok(c)], ident[0:N, 0:N]).then_inc(sm_done.sem, 1)

            def mix_xT(g, c, r=None, q=None):
                if not c:
                    wait(pe, state_ready, g - 1)
                elif q is not None:
                    wait(pe, h2T_ready, q)
                elif r is not None:
                    wait(pe, yTs_ready, r, 1)
                else:
                    wait(pe, xTs_ready, g, 1)
                for j in range(KE):
                    mm = te.transpose(B3[:, j * P:(j + 1) * P], xc[:, j, tok(c)], ident[:])
                mm.then_inc(xT_done.sem, 1)

            def mix_seg(g, c):
                wait(pe, am_ready, g, c + 1)
                if c:
                    wait(pe, E_ready, g, c)
                else:
                    wait(pe, E_ready, g - 1)
                for h in range(NH):
                    mm = te.matmul(wide[:, h * P:(h + 1) * P], am[:, h, :], tri, start=True, stop=True)
                mm.then_inc(seg_done.sem, 1)

            def mix_y(g, c, r=None, q=None):
                wait(pe, M_ready, g, c + 1)
                wait(pe, xdt_ready, g, c + 1)
                if c:
                    wait(pe, y2_done, g, c)
                    wait(pe, y1_done, g, c)
                else:
                    wait(pe, att_done, g - 1)
                for j in range(KE):
                    te.matmul(B4[:, j * P:(j + 1) * P], xc[:, j, tok(c)], diag_d[:, j, :], start=(j == 0), stop=False)
                for h in range(NH):
                    mm = te.matmul(B4[:, h * HP:(h + 1) * HP], E[c][:, h, :], xdt[:, c, h * HP:(h + 1) * HP],
                                   start=False, stop=(h == NH - 1))
                mm.then_inc(yd_done.sem, 1)
                if c:
                    wait(pe, state_ready, g, c)
                else:
                    wait(pe, state_ready, g - 1)
                    if q is not None:
                        wait(pe, lgs_ready, q)
                te.matmul(B5[:, :], CT[:, tok(c)], state, start=True, stop=True).then_inc(yo_done.sem, 1)
                wait(pe, xdd_ready, g, c + 1)
                if not c and r is not None:
                    wait(pe, yTs_ready, r)
                elif not c:
                    wait(pe, xTs_ready, g)
                te.matmul(B3[0:N, :], gb[:, c, P:P + N], xdd[:, c, :], start=True, stop=True).then_inc(sn_done.sem, 1)

            def mix_yT(r, c, g, q):
                wait(pe, yf_done, r, c + 1)
                if g is not None:
                    wait(pe, xTs_ready, g, c + 1)
                elif c:
                    wait(pe, h2T_ready, q)
                else:
                    wait(pe, state_ready, r)
                for j in range(KE):
                    mm = te.transpose(B3[:, j * P:(j + 1) * P], y[:, c, j * P:(j + 1) * P], ident[:])
                mm.then_inc(yT_done.sem, 1)

            def mix_out(g, c):
                wait(pe, yTs_ready, g, c + 1)
                if c:
                    wait(pe, att_done, g, c)
                else:
                    wait(pe, y2_done, g)
                for j in range(KE):
                    mm = te.matmul(B4[:, 0:H], yT[:, c, j * P:(j + 1) * P], wo[:, j, :], start=(j == 0), stop=(j == KE - 1))
                mm.then_inc(op_done.sem, 1)

            def route_turn(q, r):
                wait(pe, h2_ready, q)
                if r is not None:
                    wait(pe, yTs_ready, r, 1)
                for k in range(KH):
                    for c in range(G2):
                        mm = te.transpose(B3[:, k * GT + c * P:k * GT + (c + 1) * P], h2[:, c, k * P:(k + 1) * P], ident[:])
                mm.then_inc(h2T_done.sem, 1)

            def route_logits(q):
                wait(pe, h2T_ready, q)
                wait(pe, ohr_ready, q - 1)
                if isinstance(q, int):
                    wait(pe, y1_done, min(q + 1, GROUPS - 1))
                for c in range(G2):
                    for k in range(KH):
                        mm = te.matmul(B5[:, c * NE:(c + 1) * NE], h2T[:, k, tok(c)], wr[:, k, :],
                                       start=(k == 0), stop=(k == KH - 1))
                mm.then_inc(lg_done.sem, 1)

            def send(q, g):
                wait(pe, mask_ready, q)
                wait(pe, run_ready, q - 1)
                if g is not None:
                    wait(pe, y1_done, g)
                else:
                    wait(pe, lgs_ready, q)
                te.matmul(B5[:, 0:NE], before, mask[:, 0, :], start=True, stop=False)
                te.matmul(B5[:, 0:NE], ones[:], run[:], start=False, stop=True)
                te.matmul(B5[:, NE:2 * NE], before, mask[:, 1, :], start=True, stop=False)
                te.matmul(B5[:, NE:2 * NE], ones[:], mask[:, 0, :], start=False, stop=False)
                te.matmul(B5[:, NE:2 * NE], ones[:], run[:], start=False, stop=True).then_inc(rank_done.sem, 1)

            def step(s, q, r, g, f):
                if g is not None:
                    mix_small(g, 0)
                    mix_xT(g, 0)
                    mix_seg(g, 0)
                if r is not None:
                    mix_yT(r, 0, g, q)
                if g is not None:
                    mix_small(g, 1)
                if q is not None:
                    route_turn(q, r)
                if r is not None:
                    mix_out(r, 0)
                if g is not None:
                    mix_xT(g, 1, r, q)
                    mix_seg(g, 1)
                if f is not None:
                    front_zT(f)
                if q is not None:
                    route_logits(q)
                if r is not None:
                    mix_yT(r, 1, g, q)
                    mix_out(r, 1)
                if g is not None:
                    mix_y(g, 0, r, q)
                if f is not None:
                    front_conv(f)
                if g is not None:
                    mix_y(g, 1)
                if f is not None:
                    front_gate(f, 0)
                if q is not None:
                    send(q, g)
                if f is not None:
                    front_gate(f, 1)

            staggered(pe, step)

            def shared(g):
                for j in range(KS):
                    wait(pe, hid_ready, g - 1, j + 1)
                    for u in range(2):
                        for k in range(KH):
                            mm = te.matmul(up_bank[j][:, u * GT:(u + 1) * GT], wsh[:, k, u * SH + j * P:u * SH + (j + 1) * P],
                                           h2T_all[:, k, bass.ds(g * GT, GT)], start=(k == 0), stop=(k == KH - 1))
                    mm.then_inc(shp_done.sem, 1)
                wait(pe, hid_ready, g)
                for c in range(G2):
                    wait(pe, shx_ready, g - 1, c + 1)
                    for j in range(KS):
                        mm = te.matmul(wide[:, c * 512:c * 512 + H], hid[:, j, tok(c)], wsd[:, j, :],
                                       start=(j == 0), stop=(j == KS - 1))
                    mm.then_inc(shd_done.sem, 1)

            wait(pe, run_ready, GROUPS - 1)
            wait(pe, ohr_ready, GROUPS - 1)
            te.matmul(B5[:, 0:NE], ones[:], run[:], start=True, stop=True).then_inc(s_count, 1)
            wait(pe, h2T_kept, GROUPS - 1)
            pe.wait_ge(s_wsh, 32)
            shared(0)
            pe.wait_ge(s_cols, 2)
            te.matmul(B5[0:1, 0:XT], tab[:, 0:1], ident[:], start=True, stop=True)
            te.matmul(B5[0:1, XT:2 * XT], tab[:, 1:2], ident[:], start=True, stop=True).then_inc(s_tabp, 1)
            for g in range(1, EARLY):
                shared(g)

            def x_turn(i, p):
                r = i * 2 + p
                for q in range(QT):
                    wait(pe, xs_loaded[q][p], i)
                wait(pe, xsT_ready, r - 1)
                for q in range(QT):
                    for k in range(KH):
                        mm = te.transpose(wide[:, (k * QT + q) * P:(k * QT + q + 1) * P], xsb[p][:, q, k * P:(k + 1) * P], ident[:])
                mm.then_inc(xsp_done.sem, 1)

            def expert_of(r):
                return [pe.value_load(tab_i[0:1, bass.ds(r * QT + q, 1)], min_val=0, max_val=(NE - 1) * H) for q in range(QT)]

            def up(r, offs):
                wait(pe, xsT_ready, r)
                wait(pe, act_ready, r - 1)
                for q in range(QT):
                    for k in range(KH):
                        mm = te.matmul(B2[:, q * P:(q + 1) * P], xsT[:, k, q * P:(q + 1) * P],
                                       gu[:, bass.ds(offs[q] + k * P, P)], start=(k == 0), stop=(k == KH - 1))
                mm.then_inc(gup_done.sem, 1)

            def down(r, offs):
                wait(pe, aT_ready, r)
                wait(pe, ys_ready, r - 1)
                for q in range(QT):
                    mm = te.matmul((B4, B5)[q // 2][:, (q % 2) * H:(q % 2 + 1) * H], aT[:, q * P:(q + 1) * P],
                                   wd[0:FF, bass.ds(offs[q], H)], start=True, stop=True)
                    if q % 2:
                        mm.then_inc(down_done.sem, 1)

            def act_turn(r):
                wait_alone(pe, act_ready, r)
                wait_alone(pe, aT_ready, r - 1)
                for q in range(QT):
                    mm = te.transpose(B3[0:FF, q * P:(q + 1) * P], act[:, q, :], ident[:])
                mm.then_inc(aTp_done.sem, 1)

            now = [pe.alloc_register(f"now{q}") for q in range(QT)]
            before_ = [pe.alloc_register(f"before{q}") for q in range(QT)]

            def values(regs):
                return [pe.snap(reg, min_val=0, max_val=(NE - 1) * H) for reg in regs]

            def fetch_experts(r):
                for reg, off in zip(now, expert_of(r)):
                    pe.reg_mov(reg, off)

            def round_(i, p, down_before=True, more=True):
                r = i * 2 + p
                up(r, values(now))
                if more:
                    x_turn(i + p, 1 - p)
                if down_before:
                    down(r - 1, values(before_))
                for old, new in zip(before_, now):
                    pe.reg_mov(old, new)
                if more:
                    fetch_experts(r + 1)
                act_turn(r)

            pe.wait_ge(s_gu, 16)
            pe.wait_ge(s_wd, 16)
            pe.wait_ge(s_tab, 1)
            wait(pe, base_ready, EARLY - 1)
            last_i = ROUNDS // 2 - 1
            fetch_experts(0)
            x_turn(0, 0)
            round_(0, 0, down_before=False)
            with pe.Fori(0, last_i) as i:
                round_(i, 1)
                round_(i + 1, 0)
            round_(last_i, 1, more=False)
            down(ROUNDS - 1, values(before_))

            wait(pe, ys_ready, ROUNDS - 1)
            with pe.Fori(EARLY, GROUPS) as g:
                shared(g)

        @block.vector
        def _(dve):
            ve = nc.vector
            halo = cin[:, :, 0:TAPS - 1]
            ve.memset(state, 0.0).then_inc(s_vec, 1)
            ve.memset(halo, 0.0).then_inc(s_vec, 1)
            dve.wait_ge(s_csilu, 2)
            ve.tensor_scalar(neg_a, neg_a, -1.0, None, ALU.mult).then_inc(s_mod, 1)
            dve.wait_ge(s_modp, 8)
            ve.tensor_copy(col1[:, 0:KH], B2[:, 0:KH]).then_inc(s_mod, 1)
            ve.tensor_scalar(col1[:, KH:2 * KH], B2[:, KH:2 * KH], 1.0, None, ALU.add).then_inc(s_mod, 1)
            ve.tensor_copy(sb_row, B5[:, 0:H]).then_inc(s_mod, 1)
            ve.tensor_scalar(cb_row, B6[:, 0:H], 1.0, None, ALU.add).then_inc(s_mod, 1)
            for n, (b, row, tmp) in enumerate(((B4, ga_row, z1[:, 0, :]), (B7, gb_row[:], z1[:, 1, :]))):
                v = 2 + 4 * n
                ve.tensor_copy(tmp, b[:, 0:H]).then_inc(s_vec, 1)
                dve.wait_ge(s_vec, v + 1)
                ve.scalar_tensor_tensor(out=row, in0=tmp, scalar=-1.0, in1=tmp, op0=ALU.mult, op1=ALU.max).then_inc(s_vec, 1)
                dve.wait_ge(s_vec, v + 2)
                ve.tensor_scalar(row, row, 0.25, None, ALU.max).then_inc(s_vec, 1)
                ve.tensor_scalar(tmp, tmp, 0.0, 2.0, ALU.is_ge, ALU.mult).then_inc(s_vec, 1)
                dve.wait_ge(s_vec, v + 4)
                ins = ve.scalar_tensor_tensor(out=row, in0=tmp, scalar=-1.0, in1=row, op0=ALU.add, op1=ALU.mult)
                ins.then_inc(s_mod, 1)
            dve.wait_ge(s_w, 16 * (NW - 2))
            for j in range(KE):
                ve.tensor_scalar(wo[:, j, :], wo[:, j, :], nw[:, j:j + 1], None, ALU.mult).then_inc(s_mod, 1)
            dve.wait_ge(s_const, 11)
            for j in range(KE):
                ve.tensor_scalar(diag_d[:, j, :], ident[:], dcol[:, j:j + 1], None, ALU.mult).then_inc(s_mod, 1)
            dve.wait_ge(s_mod, 15)
            dve.wait_ge(s_x, 16)

            def front_stats(f):
                for c in range(G2):
                    ve.bn_stats(st6[:, c, :], x_all[:, f * G2 + c, :]).then_inc(stats1.sem, 1)
                for c in range(G2):
                    wait_alone(dve, stats1, f, c + 1)
                    ve.bn_aggr(mv1[:, c, :], st6[:, c, :]).then_inc(mv1_ready.sem, 1)
                wait(dve, mv1_ready, f)
                wait(dve, rstd1_ready, f - 1)
                ve.tensor_scalar(ve1, mv1[:, :, 1], LN_EPS, None, ALU.add).then_inc(ve1_ready.sem, 1)

            def front_z(f):
                wait(dve, rstd1_ready, f)
                wait(dve, z1T_done, f - 1)
                for c in range(G2):
                    ve.tensor_scalar(z1[:, c, :], x_all[:, f * G2 + c, :], mv1[:, c, 0:1], rstd1[:, c:c + 1],
                                     ALU.subtract, ALU.mult).then_inc(z1_ready.sem, 1)

            def front_conv(f, js):
                for k in range(1, TAPS):
                    for n, j in enumerate(js):
                        if k == 1:
                            wait(dve, tap0_done, f, j + 1)
                        else:
                            wait(dve, tap_done, f, js[0] * (TAPS - 1) + (k - 2) * len(js) + n + 1)
                        ve.scalar_tensor_tensor(out=acc[:, j, :], in0=cin[:, j, k:k + GT], scalar=cvw[:, j, k:k + 1],
                                                in1=acc[:, j, :], op0=ALU.mult, op1=ALU.add).then_inc(tap_done.sem, 1)

            def front_halo(f):
                wait(dve, tap_done, f)
                wait(dve, tap0_done, f)
                ve.tensor_copy(halo, cin[:, :, GT:]).then_inc(halo_saved.sem, 1)

            def front_dtx(f):
                wait(dve, dts_ready, f)
                wait(dve, dt_ready, f - 1)
                ve.tensor_tensor(dtx, dts, bc(r8[:, 0, :], 1, G2), ALU.add).then_inc(dtx_ready.sem, 1)
                wait(dve, dtx_ready, f, 1)
                wait(dve, dte_ready, f - 1)
                ve.scalar_tensor_tensor(out=nab, in0=dtx, scalar=-1.0, in1=dtx, op0=ALU.mult, op1=ALU.min).then_inc(dtx_ready.sem, 1)

            def front_dt(f):
                wait(dve, dte_ready, f)
                wait(dve, xdt_ready, f - 1)
                ve.scalar_tensor_tensor(out=dt, in0=dtx, scalar=0.0, in1=lnp, op0=ALU.max, op1=ALU.add)\
                  .then_inc(dt_ready.sem, 1)
                wait(dve, dt_ready, f, 1)
                wait(dve, am_ready, f - 1)
                wait(dve, sm_done, f - 1)
                ve.tensor_tensor(av, dt, bc(neg_a, 1, G2), ALU.mult).then_inc(dt_ready.sem, 1)

            def mix_M(g, c):
                wait(dve, gb_ready, g, 2 * c + 2)
                ve.tensor_tensor(gm[:, c, :], gb[:, c, 0:P], tri, ALU.mult).then_inc(gm_ready.sem, 1)
                wait(dve, gm_ready, g, c + 1)
                wait(dve, E_ready, g, c + 1)
                ve.tensor_tensor(E[c], E[c], bc(gm[:, c, :], 1, NH), ALU.mult).then_inc(M_ready.sem, 1)

            def mix_y(g, c):
                heads = lambda ap: ap.rearrange("p (h d) -> p h d", d=HP)
                wait(dve, yo_done, g, c + 1)
                wait(dve, yT_done, g - 1, c + 1)
                wait(dve, ssq_ready, g - 1, c + 1)
                ve.tensor_tensor(heads(y[:, c, :]), heads(B5[:, :]), bc(ed[:, c, 0:NH], 2, HP), ALU.mult)\
                  .then_inc(y1_done.sem, 1)
                ve.tensor_tensor(heads(state), heads(state), bc(ed[0:N, c, 2 * NH:], 2, HP), ALU.mult)\
                  .then_inc(smul_done.sem, 1)
                wait(dve, y1_done, g, c + 1)
                ve.tensor_tensor(y[:, c, :], y[:, c, :], B4[:, :], ALU.add).then_inc(y2_done.sem, 1)
                wait(dve, smul_done, g, c + 1)
                wait(dve, sn_done, g, c + 1)
                ve.tensor_tensor(state, state, B3[0:N, :], ALU.add).then_inc(state_ready.sem, 1)

            def mix_rms(g):
                wait(dve, ssq_ready, g)
                wait(dve, rstdy_ready, g - 1)
                ve.tensor_scalar(vy, ssq, 1.0 / EI, RMS_EPS, ALU.mult, ALU.add).then_inc(vy_ready.sem, 1)

            def mix_residual(g, c):
                wait(dve, op_done, g, c + 1)
                wait(dve, rstdy_ready, g)
                ve.scalar_tensor_tensor(out=x1[:, c, :], in0=B4[:, 0:H], scalar=rstdy[:, c:c + 1], in1=ga_row,
                                        op0=ALU.mult, op1=ALU.mult).then_inc(att_done.sem, 1)
                wait(dve, att_done, g, c + 1)
                ve.tensor_tensor(x1[:, c, :], x1[:, c, :], x_all[:, g * G2 + c, :], ALU.add).then_inc(x1_ready.sem, 1)

            def route_stats(g):
                for c in range(G2):
                    wait(dve, x1_ready, g, c + 1)
                    ve.bn_stats(st6b[:, c, :], x1[:, c, :]).then_inc(stats2.sem, 1)
                    ve.tensor_copy(x_all[:, g * G2 + c, :], x1[:, c, :])
                for c in range(G2):
                    wait_alone(dve, stats2, g, c + 1)
                    ve.bn_aggr(mv2[:, c, :], st6b[:, c, :]).then_inc(mv2_ready.sem, 1)
                wait(dve, mv2_ready, g)
                wait(dve, rstd2_ready, g - 1)
                ve.tensor_scalar(ve2, mv2[:, :, 1], LN_EPS, None, ALU.add).then_inc(ve2_ready.sem, 1)

            def route_norm(g):
                wait(dve, rstd2_ready, g)
                wait(dve, h2T_done, g - 1)
                wait(dve, h2s_ready, g - 1)
                for c in range(G2):
                    ve.tensor_scalar(h2[:, c, :], x1[:, c, :], mv2[:, c, 0:1], rstd2[:, c:c + 1],
                                     ALU.subtract, ALU.mult).then_inc(h2_step.sem, 1)
                for c in range(G2):
                    wait(dve, h2_step, g, c + 1)
                    ve.tensor_tensor(h2[:, c, :], h2[:, c, :], cb_row, ALU.mult).then_inc(h2_step.sem, 1)
                for c in range(G2):
                    wait(dve, h2_step, g, c + 3)
                    ve.tensor_tensor(h2[:, c, :], h2[:, c, :], sb_row, ALU.add).then_inc(h2_ready.sem, 1)

            def route(g):
                wait(dve, lg_done, g)
                wait(dve, el_ready, g - 1)
                ve.tensor_copy(lgs, B5[:, 0:G2 * NE].rearrange("p (c e) -> p c e", c=G2)).then_inc(lgs_ready.sem, 1)
                wait(dve, lgs_ready, g)
                ve.tensor_tensor(lb, lgs, bc(rb, 1, G2), ALU.add).then_inc(lb_ready.sem, 1)
                ve.tensor_reduce(nm, lgs, AX.X, ALU.max, negate=True).then_inc(nm_ready.sem, 1)
                wait_alone(dve, lb_ready, g)
                for c in range(G2):
                    ve.max(m8[:, c, :], lb[:, c, :]).then_inc(m8_ready.sem, 1)
                for c in range(G2):
                    wait_alone(dve, m8_ready, g, c + 1)
                    ve.max_index(ix8[:, c, :], m8[:, c, :], lb[:, c, :]).then_inc(ix_ready.sem, 1)
                wait(dve, ix_ready, g)
                four = lambda ap: ap.rearrange("p (c k) -> p c k", c=G2)
                ve.tensor_copy(four(ixf), ix8[:, :, 0:TOP]).then_inc(ixf_ready.sem, 1)
                wait(dve, ixf_ready, g)
                ve.tensor_tensor(oh, iota8, bc(ixf, 2, NE), ALU.is_equal).then_inc(oh_ready.sem, 1)
                ve.tensor_copy(idx_all[:, bass.ds(g * (G2 * TOP), G2 * TOP)], ixf)
                wait(dve, oh_ready, g)
                wait(dve, run_ready, g - 1)
                ve.tensor_reduce(mask, oh.rearrange("p (c k) e -> p c e k", c=G2), AX.X, ALU.add).then_inc(mask_ready.sem, 1)

            def weigh(g):
                four = lambda ap: ap.rearrange("p (c k) -> p c k", c=G2)
                wait(dve, el_ready, g)
                o4 = lambda ap: ap.rearrange("p (c k) e -> p c k e", c=G2)
                ve.tensor_tensor(o4(ohe), o4(oh), bc(el, 2, TOP), ALU.mult).then_inc(cw_steps.sem, 1)
                wait(dve, cw_steps, g, 1)
                ve.tensor_reduce(cw, ohe, AX.X, ALU.add).then_inc(cw_steps.sem, 1)
                wait(dve, cw_steps, g, 2)
                ve.tensor_reduce(csum, four(cw), AX.X, ALU.add).then_inc(cw_steps.sem, 1)
                wait(dve, cw_steps, g, 3)
                ve.reciprocal(rcs, csum).then_inc(cw_steps.sem, 1)
                wait(dve, cw_steps, g, 4)
                ve.tensor_tensor(four(cw_all[:, bass.ds(g * (G2 * TOP), G2 * TOP)]), four(cw), bc(rcs, 2, TOP), ALU.mult)\
                  .then_inc(cw_steps.sem, 1)

            def send(q):
                o4 = lambda ap: ap.rearrange("p (c k) e -> p c k e", c=G2)
                wait(dve, rank_done, q)
                ve.tensor_tensor(o4(ohr), o4(oh), bc(B5[:, 0:G2 * NE].rearrange("p (c e) -> p c e", c=G2), 2, TOP), ALU.mult)\
                  .then_inc(ohr_ready.sem, 1)
                wait(dve, ohr_ready, q)
                ve.tensor_reduce(rank, ohr, AX.X, ALU.add).then_inc(rank_ready.sem, 1)
                wait(dve, rank_ready, q)
                wait(dve, rows_free, q - 1)
                ve.scalar_tensor_tensor(out=pos, in0=ixf, scalar=float(REGION), in1=rank, op0=ALU.mult, op1=ALU.add)\
                  .then_inc(pos_ready.sem, 1)
                ve.tensor_copy(rank_all[:, bass.ds(q * (G2 * TOP), G2 * TOP)], rank)
                wait(dve, h2_ready, q)
                ve.tensor_copy(h2s, h2).then_inc(h2s_ready.sem, 1)

            def step(s, q, r, g, f):
                if f is not None:
                    front_stats(f)
                if r is not None:
                    mix_rms(r)
                if f is not None:
                    front_z(f)
                if g is not None:
                    mix_M(g, 0)
                if r is not None:
                    mix_residual(r, 0)
                if g is not None:
                    mix_M(g, 1)
                if q is not None:
                    route(q)
                if r is not None:
                    mix_residual(r, 1)
                    route_stats(r)
                if g is not None:
                    mix_y(g, 0)
                if f is not None:
                    front_conv(f, (0, 1))
                    front_conv(f, (2, 3))
                    front_dtx(f)
                    front_conv(f, (4,))
                    front_halo(f)
                if g is not None:
                    mix_y(g, 1)
                if f is not None:
                    front_dt(f)
                if q is not None:
                    weigh(q)
                    send(q)
                if r is not None:
                    route_norm(r)

            staggered(dve, step)

            dve.wait_ge(s_count, 1)
            plan = [0]

            def planned(ins):
                plan[0] += 1
                ins.then_inc(s_plan, 1)
                dve.wait_ge(s_plan, plan[0])

            planned(ve.tensor_copy(cnt[:], B5[:, 0:NE]))
            planned(ve.memset(one_e[:], 1.0))
            planned(ve.tensor_scalar(cnt_i[:], cnt[:], float(P - 1), None, ALU.add))
            planned(ve.tensor_scalar(nt_i[:], cnt_i[:], P.bit_length() - 1, None, ALU.arith_shift_right))
            planned(ve.tensor_copy(ntf[:], nt_i[:]))
            planned(ve.tensor_tensor_scan(tend[:], one_e[:], ntf[:], 0.0, ALU.mult, ALU.add))
            planned(ve.tensor_tensor(tstart[:], tend[:], ntf[:], ALU.subtract))
            planned(ve.tensor_scalar(last[:], cnt[:], float(-P), 0.0, ALU.add, ALU.max))
            planned(ve.scalar_tensor_tensor(out=pack[:], in0=tstart[:], scalar=float(2 * S), in1=cnt[:], op0=ALU.mult, op1=ALU.add))
            dve.wait_ge(s_const, 11)
            planned(ve.tensor_scalar(le[:], tend[:], pidx[:, 0:1], 0.0, ALU.is_le, ALU.add, accum_out=tab[:, 2:3]))
            planned(ve.tensor_scalar(tab[:, 3:4], tab[:, 2:3], float(NE), None, ALU.is_lt))
            planned(ve.scalar_tensor_tensor(out=le[:], in0=iota_e[:], scalar=tab[:, 2:3], in1=tstart[:], op0=ALU.is_equal,
                                            op1=ALU.mult, accum_out=tab[:, 4:5]))
            planned(ve.scalar_tensor_tensor(out=le[:], in0=iota_e[:], scalar=tab[:, 2:3], in1=last[:], op0=ALU.is_equal,
                                            op1=ALU.mult, accum_out=tab[:, 8:9]))
            planned(ve.tensor_scalar(tab[:, 5:6], pidx[:, 0:1], tab[:, 4:5], float(P), ALU.subtract, ALU.mult))
            planned(ve.tensor_tensor(tab[:, 9:10], tab[:, 5:6], tab[:, 8:9], ALU.min))
            planned(ve.scalar_tensor_tensor(out=tab[:, 10:11], in0=tab[:, 2:3], scalar=float(REGION), in1=tab[:, 9:10],
                                            op0=ALU.mult, op1=ALU.add))
            ve.tensor_scalar(tab[:, 0:1], tab[:, 2:3], tab[:, 3:4], float(KH * P), ALU.mult, ALU.mult).then_inc(s_cols, 1)
            ve.tensor_scalar(tab[:, 1:2], tab[:, 10:11], tab[:, 3:4], None, ALU.mult).then_inc(s_cols, 1)

            def shared_hidden(g):
                for j in range(KS):
                    wait(dve, shg_ready, g, j + 1)
                    wait(dve, shd_done, g - 1)
                    ve.tensor_tensor(hid[:, j, :], shg[:, j, :], up_bank[j][:, GT:], ALU.mult).then_inc(hid_ready.sem, 1)

            def shared_sum(g):
                for c in range(G2):
                    wait(dve, shd_done, g, c + 1)
                    wait(dve, base_ready, g - 1)
                    ve.tensor_tensor(sh_x[:, c, :], wide[:, c * 512:c * 512 + H], gb_row[:], ALU.mult)\
                      .then_inc(shx_ready.sem, 1)
                for c in range(G2):
                    wait(dve, shx_ready, g, c + 1)
                    ve.tensor_tensor(x_all[:, g * G2 + c, :], sh_x[:, c, :], x_all[:, g * G2 + c, :], ALU.add)\
                      .then_inc(base_ready.sem, 1)

            wait(dve, xc_ready, GROUPS - 1)
            wait(dve, gatep_done, GROUPS - 1)
            shared_hidden(0)
            shared_sum(0)
            dve.wait_ge(s_tabp, 1)
            ve.tensor_copy(tab_i[0:1, :], B5[0:1, 0:2 * XT]).then_inc(s_tab, 1)
            for g in range(1, EARLY):
                shared_hidden(g)
                shared_sum(g)
            wait(dve, scattered, GROUPS - 1)

            def x_copy(r):
                wait(dve, xsp_done, r)
                wait(dve, gup_done, r - 1)
                ve.tensor_copy(xsT[:, 1, :], wide[:, QT * P:]).then_inc(xsT_ready.sem, 1)

            def choose(r, p):
                wait(dve, sel_steps, r - 1)
                ve.tensor_tensor(selw[0], bc(iota_e[:], 1, 2), bc(idx_all[:, bass.ds(r * 2, 2)], 2, NE), ALU.is_equal)\
                  .then_inc(sel_steps.sem, 1)

            def chosen(r, k):
                wait(dve, sel_steps, r, k)
                if k == 1:
                    ve.tensor_tensor(selw[1], selw[0], bc(pack[:], 1, 2), ALU.mult).then_inc(sel_steps.sem, 1)
                else:
                    ve.tensor_reduce(pk_all[:, bass.ds(r * 2, 2)], selw[1], AX.X, ALU.add).then_inc(sel_steps.sem, 1)

            def round_(i, p, more=True):
                r = i * 2 + p
                choose(r, p)
                wait(dve, sg_ready, r)
                wait(dve, aTp_done, r - 1)
                ve.tensor_tensor(act, sg, B2[:, :].rearrange("p (q f) -> p q f", q=QT)[:, :, FF:], ALU.mult)\
                  .then_inc(act_ready.sem, 1)
                if more:
                    x_copy(r + 1)
                chosen(r, 1)

            def tail(i, p):
                r = i * 2 + p
                wait(dve, aTp_done, r)
                wait(dve, down_done, r - 1)
                ve.tensor_copy(aT, B3[0:FF, :]).then_inc(aT_ready.sem, 1)
                chosen(r, 2)

            def rows_out(i, p):
                r = i * 2 + p
                wait(dve, down_done, r)
                wait(dve, ys_stored[p], i - 1)
                ve.tensor_copy(ysb[p][:, 2:4, :], B5[:, :].rearrange("p (q d) -> p q d", q=2)).then_inc(ys_ready.sem, 1)

            last_i = ROUNDS // 2 - 1
            def two_rounds(i):
                round_(i, 1)
                rows_out(i, 0)
                tail(i, 1)
                round_(i + 1, 0)
                rows_out(i, 1)
                tail(i + 1, 0)

            x_copy(0)
            round_(0, 0)
            tail(0, 0)
            two_rounds(0)
            with dve.Fori(1, last_i) as i:
                two_rounds(i)
            round_(last_i, 1, more=False)
            rows_out(last_i, 0)
            tail(last_i, 1)

            done = [0]

            def stepped(ins):
                done[0] += 1
                ins.then_inc(s_sel, 1)
                dve.wait_ge(s_sel, done[0])

            bits = (2 * S).bit_length() - 1
            wait(dve, sel_steps, ROUNDS - 1)
            stepped(ve.tensor_copy(pk_i, pk_all[:]))
            stepped(ve.tensor_scalar(st_i, pk_i, bits, None, ALU.arith_shift_right))
            stepped(ve.tensor_scalar(n_i, pk_i, 2 * S - 1, None, ALU.bitwise_and))
            stepped(ve.tensor_copy(st_f, st_i))
            stepped(ve.tensor_scalar(n_f, n_i, float(-P), 0.0, ALU.add, ALU.max))
            stepped(ve.tensor_tensor(inlast, rank_all[:], n_f, ALU.is_ge))
            stepped(ve.tensor_scalar(n_i, n_f, -1.0, float(4 * S), ALU.mult, ALU.add))
            stepped(ve.tensor_scalar(n_i, n_i, P - 1, None, ALU.bitwise_and))
            stepped(ve.tensor_tensor(back, inlast, n_i, ALU.mult))
            stepped(ve.scalar_tensor_tensor(out=st_f, in0=st_f, scalar=float(P), in1=rank_all[:], op0=ALU.mult, op1=ALU.add))
            stepped(ve.tensor_tensor(pos2, st_f, back, ALU.add))
            rows_out(last_i, 1)

            def gather(i, p):
                g = i * 2 + p
                for c in range(G2):
                    for k in range(TOP):
                        j = c * TOP + k
                        wait(dve, gathered[j][p], i)
                        if k:
                            wait(dve, comb_ready, g, j)
                            ve.scalar_tensor_tensor(out=comb[:, c, :], in0=yg[p][:, j, :],
                                                    scalar=cw_all[:, bass.ds(g * (G2 * TOP) + j, 1)],
                                                    in1=comb[:, c, :], op0=ALU.mult, op1=ALU.add).then_inc(comb_ready.sem, 1)
                        else:
                            wait(dve, fin_steps, g - 1)
                            ve.tensor_scalar(comb[:, c, :], yg[p][:, j, :], cw_all[:, bass.ds(g * (G2 * TOP) + j, 1)], None,
                                             ALU.mult).then_inc(comb_ready.sem, 1)
                for c in range(G2):
                    wait(dve, comb_ready, g, (c + 1) * TOP)
                    wait(dve, fin_free, g - 1)
                    ve.tensor_tensor(fin[:, c, :], comb[:, c, :], gb_row[:], ALU.mult).then_inc(fin_steps.sem, 1)
                for c in range(G2):
                    wait(dve, fin_steps, g, c + 1)
                    ve.tensor_tensor(fin[:, c, :], fin[:, c, :], x_all[:, g * G2 + c, :], ALU.add).then_inc(fin_ready.sem, 1)

            with dve.Fori(EARLY // 2, GROUPS // 2) as i:
                for p in range(2):
                    shared_hidden(i * 2 + p)
                    gather(i - EARLY // 2, p)
                    shared_sum(i * 2 + p)
            for i in range((GROUPS - EARLY) // 2, GROUPS // 2):
                for p in range(2):
                    gather(i, p)


def kernel(L0_attn_x, L0_attn_in_proj_w, L0_attn_conv_w, L0_attn_conv_b, L0_attn_dt_bias, L0_attn_A_log, L0_attn_D,
           L0_attn_norm_w, L0_attn_out_proj_w, L0_ffn_router_w, L0_ffn_router_bias, L0_ffn_wg, L0_ffn_wu, L0_ffn_wd,
           L0_ffn_swg, L0_ffn_swu, L0_ffn_swd, L0_c, L0_wmod):
    import numpy as np
    import concourse.bacc as bacc
    from concourse.bass_utils import run_bass_kernel_spmd as run_kernel

    arr = np.asarray

    def rows(v):
        return np.broadcast_to(arr(v)[None, :], (P, arr(v).shape[0]))

    def columns(v):
        return arr(v).reshape(-1, P).T

    conv = np.concatenate([arr(L0_attn_conv_w), arr(L0_attn_conv_b)[:, None]], axis=1)
    gu = np.concatenate([arr(L0_ffn_wg), arr(L0_ffn_wu)], axis=2)
    shared = [arr(w).transpose(1, 0, 2).reshape(H, SH) for w in (L0_ffn_swg, L0_ffn_swu)]
    data = {
        "x": arr(L0_attn_x).reshape(S, H),
        "w_in": arr(L0_attn_in_proj_w).T,
        "conv": conv.reshape(CJ, P, TAPS + 1).transpose(1, 0, 2),
        "rows8": np.stack([rows(v) for v in (L0_attn_dt_bias, L0_attn_A_log)], axis=1),
        "norm_w": columns(L0_attn_norm_w),
        "w_out": arr(L0_attn_out_proj_w).T,
        "w_router": arr(L0_ffn_router_w),
        "rbias": rows(L0_ffn_router_bias),
        "w_gu": gu.reshape(NE, KH, P, 2 * FF).transpose(2, 0, 1, 3).reshape(P, NE * KH * 2 * FF),
        "w_d": arr(L0_ffn_wd).transpose(1, 0, 2).reshape(FF, NE * H),
        "w_sgu": np.concatenate(shared, axis=1),
        "w_sd": arr(L0_ffn_swd).reshape(SH, H),
        "cvec": columns(arr(L0_c)[0]),
        "w_mod": arr(L0_wmod),
        "d_cols": columns(np.repeat(arr(L0_attn_D), HP)),
    }
    data = {n: np.ascontiguousarray(v) for n, v in data.items()}
    nc = bacc.Bacc("TRN2", target_bir_lowering=False, num_devices=1)
    args = [nc.dram_tensor(n, v.shape, F32, kind="ExternalInput").ap() for n, v in data.items()]
    args.append(nc.dram_tensor("out", (S, H), F32, kind="ExternalOutput").ap())
    build(nc, *args)
    return run_kernel(nc, [data], core_ids=[0]).results[0]["out"].reshape(1, S, H)
```
